# Optimizing a Trainium2 kernel written in Bass

```python
import numpy as np
import jax
import jax.numpy as jnp

def _softmax(x, axis=-1):
    return jax.nn.softmax(x, axis=axis)

def _gelu(x):
    return jax.nn.gelu(x, approximate=True)

def _silu(x):
    return jax.nn.silu(x)

def _sigmoid(x):
    return jax.nn.sigmoid(x)

def _layernorm(x, axis=-1, eps=1e-05):
    m = jnp.mean(x, axis=axis, keepdims=True)
    v = jnp.var(x, axis=axis, keepdims=True)
    return (x - m) / jnp.sqrt(v + eps)

def _scatter_add(tgt, idx, src, axis=0):
    return tgt.at[idx].add(src)

def _segment_sum(src, seg, n):
    return jax.ops.segment_sum(src, seg, n)
kernel_name = 'mk_xattn_ffn_d1_seqx_r4_346291'

def setup_inputs(seed: int=0):
    np.random.seed(seed)
    _w = jnp.asarray

    def _rec_inputs():
        import jax
        import jax.numpy as jnp
        _rk = jax.random.key(seed)
        x = 0.5 + 0.2887 * jax.random.normal(jax.random.fold_in(_rk, 1), (4, 512, 512), jnp.float32)
        _lenS = 512 - jax.random.randint(jax.random.fold_in(_rk, 7), (4,), 0, max(1, 512 // 4) + 1, jnp.int32)
        _lenS2 = 512 - jax.random.randint(jax.random.fold_in(_rk, 8), (4,), 0, max(1, 512 // 4) + 1, jnp.int32)
        _ctx_512P = jax.random.normal(jax.random.fold_in(_rk, 11), (4, 16, 128), jnp.float32)
        _ctx_512c = jax.random.dirichlet(jax.random.fold_in(_rk, 511), 0.3 * jnp.ones((16,), jnp.float32), (4, 512))
        _ctx_512t = jnp.einsum('bsk,bkd->bsd', _ctx_512c, _ctx_512P)
        _ctx_512t = _ctx_512t * jax.lax.rsqrt(jnp.mean(jnp.square(_ctx_512t)) + 1e-12) * 0.953939
        ctx_512 = -0.000392918 + 0.999932 * (_ctx_512t + 0.3 * jax.random.normal(jax.random.fold_in(_rk, 611), (4, 512, 128), jnp.float32))
        return (x, ctx_512)
    x, ctx_512 = _rec_inputs()

    def _L0_xattn_setup():
        import jax, jax.numpy as jnp
        import numpy as np
        B, N, D = (16, 512, 128)
        H = 4
        TOP_K_RATIO = 0.3
        key = jax.random.key(seed)
        k1, k2, k3, k4 = jax.random.split(key, 4)
        h = jax.random.normal(k1, (B, N, D), dtype=jnp.float32)
        adj_raw = jax.random.uniform(k2, (B, N, N), dtype=jnp.float32)
        lim = 1.0 / np.sqrt(D)
        Wq = jax.random.uniform(k3, (D, D), minval=-lim, maxval=lim, dtype=jnp.float32)
        Wk = jax.random.uniform(k4, (D, D), minval=-lim, maxval=lim, dtype=jnp.float32)
        gamma_raw = jnp.float32(-0.85)
        return {'h': h, 'adj_raw': adj_raw, 'Wq': Wq, 'Wk': Wk, 'gamma_raw': gamma_raw}
    _L0_xattn_all = _L0_xattn_setup()
    _L0_xattn_in = {k: v for k, v in _L0_xattn_all.items() if k in ('Wq', 'Wk', 'gamma_raw')}
    del _L0_xattn_all

    def _L0_ffn_setup():
        import jax, jax.numpy as jnp
        import numpy as np
        EPS = 1e-05
        TOP_K = 2

        def weight_quant(w):
            scale = 1.0 / jnp.maximum(jnp.mean(jnp.abs(w)), EPS)
            return jnp.clip(jnp.round(w * scale), -1.0, 1.0) / scale

        def activation_quant(x):
            scale = 127.0 / jnp.maximum(jnp.max(jnp.abs(x), axis=-1, keepdims=True), EPS)
            return jnp.clip(jnp.round(x * scale), -128.0, 127.0) / scale

        def bitlinear(x, w):
            w_q = w + jax.lax.stop_gradient(weight_quant(w) - w)
            x_q = x + jax.lax.stop_gradient(activation_quant(x) - x)
            return x_q @ w_q.T

        def expert_ffn(x, gw, uw, dw):
            gate = bitlinear(x, gw)
            up = bitlinear(x, uw)
            activated = up * jnp.square(jax.nn.relu(gate))
            return bitlinear(activated, dw)
        key = jax.random.key(seed)
        ks = jax.random.split(key, 5)
        B, S, H, I, E = (2, 512, 512, 1024, 8)
        return {'hidden_states': jax.random.normal(ks[0], (B, S, H), dtype=jnp.float32), 'router_w': jax.random.normal(ks[1], (E, H), dtype=jnp.float32) * 0.02, 'gate_w': jax.random.normal(ks[2], (E, I, H), dtype=jnp.float32) * 0.02, 'up_w': jax.random.normal(ks[3], (E, I, H), dtype=jnp.float32) * 0.02, 'down_w': jax.random.normal(ks[4], (E, H, I), dtype=jnp.float32) * 0.02}
    _L0_ffn_all = _L0_ffn_setup()
    _L0_ffn_in = {k: v for k, v in _L0_ffn_all.items() if k in ('router_w', 'gate_w', 'up_w', 'down_w')}
    del _L0_ffn_all
    return {'x': x, 'ctx_512': ctx_512, 'L0_xattn_Wq': _L0_xattn_in['Wq'], 'L0_xattn_Wk': _L0_xattn_in['Wk'], 'L0_xattn_gamma_raw': _L0_xattn_in['gamma_raw'], 'L0_ffn_router_w': _L0_ffn_in['router_w'], 'L0_ffn_gate_w': _L0_ffn_in['gate_w'], 'L0_ffn_up_w': _L0_ffn_in['up_w'], 'L0_ffn_down_w': _L0_ffn_in['down_w']}

def reference(x, ctx_512, L0_xattn_Wq, L0_xattn_Wk, L0_xattn_gamma_raw, L0_ffn_router_w, L0_ffn_gate_w, L0_ffn_up_w, L0_ffn_down_w):
    import jax
    import jax.numpy as jnp

    def _L0_xattn_ref(h, adj_raw, Wq, Wk, gamma_raw):
        import jax, jax.numpy as jnp
        import numpy as np
        B, N, D = (16, 512, 128)
        H = 4
        TOP_K_RATIO = 0.3
        b, n, dm = h.shape
        d = dm // H
        Q = (h @ Wq.T).reshape(b, n, H, d).transpose(0, 2, 1, 3)
        K = (h @ Wk.T).reshape(b, n, H, d).transpose(0, 2, 1, 3)
        sim = jnp.einsum('bhnd,bhmd->bnm', Q, K) / (jnp.sqrt(jnp.float32(d)) * H)
        k = max(1, int(n * TOP_K_RATIO))
        topk_vals = jax.lax.top_k(sim, k)[0]
        threshold = topk_vals[:, :, -1:]
        sparse_mask = (sim >= threshold).astype(sim.dtype)
        A_learned = jax.nn.sigmoid(sim) * sparse_mask
        A_learned = (A_learned + jnp.swapaxes(A_learned, -1, -2)) * 0.5
        gamma = jax.nn.sigmoid(gamma_raw)
        return (1.0 - gamma) * adj_raw + gamma * A_learned

    def _L0_ffn_ref(hidden_states, router_w, gate_w, up_w, down_w):
        import jax, jax.numpy as jnp
        import numpy as np
        EPS = 1e-05
        TOP_K = 2

        def weight_quant(w):
            scale = 1.0 / jnp.maximum(jnp.mean(jnp.abs(w)), EPS)
            return jnp.clip(jnp.round(w * scale), -1.0, 1.0) / scale

        def activation_quant(x):
            scale = 127.0 / jnp.maximum(jnp.max(jnp.abs(x), axis=-1, keepdims=True), EPS)
            return jnp.clip(jnp.round(x * scale), -128.0, 127.0) / scale

        def bitlinear(x, w):
            w_q = w + jax.lax.stop_gradient(weight_quant(w) - w)
            x_q = x + jax.lax.stop_gradient(activation_quant(x) - x)
            return x_q @ w_q.T

        def expert_ffn(x, gw, uw, dw):
            gate = bitlinear(x, gw)
            up = bitlinear(x, uw)
            activated = up * jnp.square(jax.nn.relu(gate))
            return bitlinear(activated, dw)
        B, S, H = hidden_states.shape
        E = router_w.shape[0]
        x = hidden_states.reshape(-1, H)
        logits = x @ router_w.T
        probs = jax.nn.softmax(logits, axis=-1)
        top_w, top_i = jax.lax.top_k(probs, TOP_K)
        top_w = top_w / jnp.sum(top_w, axis=-1, keepdims=True)
        combine = jnp.sum(top_w[..., None] * jax.nn.one_hot(top_i, E, dtype=x.dtype), axis=1)
        out = jnp.zeros_like(x)
        for e in range(E):
            y_e = expert_ffn(x, gate_w[e], up_w[e], down_w[e])
            out = out + combine[:, e:e + 1] * y_e
        return out.reshape(B, S, H)
    x = x + _L0_xattn_ref(ctx_512, _layernorm(x, axis=-1), L0_xattn_Wq, L0_xattn_Wk, L0_xattn_gamma_raw)
    x = x + _L0_ffn_ref(_layernorm(x, axis=-1), L0_ffn_router_w, L0_ffn_gate_w, L0_ffn_up_w, L0_ffn_down_w)
    return x

_drawn_inputs = setup_inputs


def setup_inputs(seed=0):
    import zlib

    import numpy as np

    out = dict(_drawn_inputs(seed))
    spreads = {}
    factors = {'L0_ffn_router_w': 7.466,
     'L0_ffn_gate_w': 6.993,
     'L0_ffn_up_w': 6.399,
     'L0_ffn_down_w': 6.391}
    for name, (base, spread) in spreads.items():
        noise = np.random.default_rng([zlib.crc32(name.encode()), seed]).standard_normal(out[name].shape)
        drawn = base * np.exp(spread * noise) if base else spread * noise
        out[name] = jnp.asarray(drawn.astype(out[name].dtype))
    for name, factor in factors.items():
        out[name] = (out[name] * factor).astype(out[name].dtype)
    return out
```

```python
from contextlib import ExitStack

import concourse.bass as bass
from concourse import mybir
from concourse.alu_op_type import AluOpType as ALU

F32, BF16, I32, I8 = mybir.dt.float32, mybir.dt.bfloat16, mybir.dt.int32, mybir.dt.int8
ACT = mybir.ActivationFunctionType
AX = mybir.AxisListType
P = 128
EPS = 1e-5
MAGIC = 1.5 * 2.0 ** 23
LOWEST = -3.0e38


class Chain:

    def __init__(self, eng, sem):
        self.eng, self.sem, self.n = eng, sem, 0

    def __call__(self, ins):
        self.note(ins)
        self.settle()

    def note(self, ins):
        ins.then_inc(self.sem, 1)
        self.n += 1

    def settle(self):
        self.eng.wait_ge(self.sem, self.n)

    def after(self, mark):
        self.eng.wait_ge(self.sem, mark)

    def restart(self):
        self.settle()
        self.eng.sem_clear(self.sem)
        self.n = 0


def build(nc, x, ctxT, wqT, wkT, gamma, routerT, gateT, upT, downT, out):
    B, N, H = x.shape
    D = wqT.shape[0]
    E = routerT.shape[-1]
    I = gateT.shape[-1]
    RT = N // P
    KH, KI = H // P, I // P
    T = B * N
    TT = T // P
    TOPK = 2
    KEEP = max(1, int(N * 0.3))
    ROUNDS = -(-KEEP // 8)
    LOW_END, HIGH_END = (-0.4, 0.4383 * N), (1.3, 0.1758 * N)
    COUNTS = 5
    TARGET = KEEP - 4.5
    TILES = T * TOPK // P + E - 1
    ROW = H // 2 + 3
    SCALE, TOKEN, WEIGHT = H // 2, H // 2 + 1, H // 2 + 2
    MATS = 3
    WLEN = KH * I
    NW = E * MATS
    STAGES = 3
    ARENA = 13360
    SIM_SCALE = 1.0 / (float((D // 4) ** 0.5) * 4)

    xs = nc.dram_tensor("routed_rows", [TILES * P, ROW], F32)
    sums = out
    x_t = x.rearrange("b (t p) h -> (b t) p h", p=P)
    weights_dram = tuple(w.rearrange("e p k n -> e p (k n)") for w in (gateT, upT, downT))

    ctx = ExitStack()
    with ctx:
        def sb(name, shape, dt=F32):
            return ctx.enter_context(nc.sbuf_tensor(name, shape, dt))

        def sem(name):
            return ctx.enter_context(nc.semaphore(name))

        bank = [ctx.enter_context(nc.psum_tensor(f"bank{i}", [P, 512], F32)) for i in range(8)]

        w8 = sb("w8", [P, NW, WLEN], I8)
        arena_w = sb("arena_w", [P, 2 * MATS * WLEN], BF16)
        arena = sb("arena", [P, ARENA], F32)
        ident_f = sb("ident_f", [P, P])
        ident_b = sb("ident_b", [P, P], BF16)
        tri_b = sb("tri_b", [P, P], BF16)
        ones_b = sb("ones_b", [P, P], BF16)
        ones_f = sb("ones_f", [P, P])
        wq_sb = sb("wq_sb", [P, P])
        wk_sb = sb("wk_sb", [P, P])
        router_sb = sb("router_sb", [P, KH, E])
        g_raw = sb("g_raw", [P, 1])
        g_sig = sb("g_sig", [P, 1])
        g_half = sb("g_half", [P, 1])
        g_rest = sb("g_rest", [P, 1])
        abs_part = sb("abs_part", [P, NW])
        wmean = sb("wmean", [P, NW])
        wscale = sb("wscale", [P, NW])
        iota_i = sb("iota_i", [P, E + 1 + TILES], I32)
        iota_e = sb("iota_e", [P, E])
        iota_p = sb("iota_p", [P, 1])
        iota_t = sb("iota_t", [P, TILES])
        g_ident = sb("g_ident", [P, P])
        first_row = sb("first_row", [P, E])
        slots = sb("slots", [P, TT, TOPK], I32)
        combine = sb("combine", [P, TT, TOPK])
        fill_rows = sb("fill_rows", [P, ROW])
        tokens = sb("tokens", [P, TILES], I32)
        tile_tokens = [sb(f"tile_tokens{u}", [P, 1], I32) for u in range(2)]
        tab = sb("tab", [P, TILES])
        past = sb("past", [P, TILES, E - 1])
        tab_i = sb("tab_i", [P, TILES], I32)
        ends = sb("ends", [P, 3, E])
        ends_i = sb("ends_i", [P, 2, E], I32)
        expert_c = sb("expert_c", [P, E])
        expert_d = sb("expert_d", [P, E])
        small = sb("small", [P, 8, TT])
        m_b = sb("m_b", [P, TT, E], BF16)
        st = sb("st", [P, 2, TT, 6])
        mean = sb("mean", [P, 2, TT])
        var = sb("var", [P, 2, TT])
        nw = sb("nw", [P, 4, 2, TT])
        rstd = sb("rstd", [P, 2, TT])
        a1 = sb("a1", [P, TT])
        b1 = sb("b1", [P, TT])
        a_ln2 = sb("a_ln2", [P, TT])
        b_ln2 = sb("b_ln2", [P, TT])
        now = sb("now", [P, 2, TT])
        low = sb("low", [P, 2, TT])
        high = sb("high", [P, 2, TT])
        span = sb("span", [P, 2, TT])
        side = sb("side", [P, 2, TT], I32)
        place = sb("place", [P, TT])
        bad = sb("bad", [P, TT])
        flags_i = sb("flags_i", [P, TT + 1], I32)
        kept_less = sb("kept_less", [P, 1])
        m8 = sb("m8", [P, RT, 8])
        pick = sb("pick", [P, 2, RT, 8])
        thr = sb("thr", [P, RT])
        hm = sb("hm", [P, 4, RT])
        stage = [arena_w[:, 2 * s * WLEN:2 * (s + 1) * WLEN].bitcast(F32) for s in range(STAGES)]
        slot_w = arena_w[:, :]

        used = [0]

        def carve(n):
            o = used[0]
            used[0] += n
            assert used[0] <= ARENA, used[0]
            return arena[:, o:o + n]

        x_all = carve(TT * H).rearrange("p (t h) -> p t h", t=TT)
        scratch = used[0]
        qk_at = used[0]
        q_sb = [carve(N) for _ in range(2)]
        k_sb = [carve(N) for _ in range(2)]
        sig = carve(RT * N).rearrange("p (t n) -> p t n", t=RT)
        ctx_sb = [carve(N) for _ in range(2)]
        junk = [sig[:, t, :] for t in range(RT)]
        w_junk = arena[:, qk_at:qk_at + WLEN // 4].bitcast(I8)
        used[0] = scratch
        xq_f = carve(TT * ROW).rearrange("p (t h) -> p t h", t=TT)
        xq = xq_f.bitcast(BF16)
        hT = [carve(H).rearrange("p (k n) -> p k n", k=KH) for _ in range(2)]
        used[0] = 0
        rt = carve(14 * TT * E).rearrange("p (n t e) -> p n t e", n=14, t=TT)
        h_sb = [w8[:, NW - 4 + 2 * u:NW - 2 + 2 * u, :].rearrange("p k w -> p (k w)").bitcast(F32)
                .rearrange("p (t h) -> p t h", t=RT) for u in range(2)]
        SIM_MATS = TT * N * 4 // WLEN
        sim = w8[:, NW - SIM_MATS:NW, :].rearrange("p k w -> p (k w)").bitcast(F32).rearrange(
            "p (t n) -> p t n", t=TT)
        below = ctx_sb
        diag = k_sb[0].rearrange("p (t n) -> p t n", t=RT)

        used[0] = 0
        xr_f = [carve(ROW) for _ in range(2)]
        xr = [v.bitcast(BF16) for v in xr_f]
        xT = [carve(H // 2).bitcast(BF16).rearrange("p (k n) -> p k n", k=KH) for _ in range(2)]
        relu_sb = [carve(512) for _ in range(2)]
        sq_sb = [carve(512) for _ in range(2)]
        act_sb = carve(I)
        act_r = carve(I)
        aq = [carve(I // 2).bitcast(BF16) for _ in range(2)]
        aT = [carve(I // 2).bitcast(BF16).rearrange("p (k n) -> p k n", k=KI) for _ in range(2)]
        y_sb = [carve(H) for _ in range(2)]
        fs = [carve(1) for _ in range(2)]
        osc = [carve(1) for _ in range(2)]
        weight = [carve(1) for _ in range(2)]
        tiny = carve(4)

        s_const_in = sem("const_in")
        s_masks = sem("masks_made")
        s_pool_order = sem("pool_order")
        s_dve_order = sem("dve_order")
        s_act_order = sem("act_order")
        s_ctx_in = [sem(f"ctx_in{u}") for u in range(2)]
        s_x_in = [sem(f"x_in{u}") for u in range(2)]
        s_w_in = [sem(f"weights_in{s}") for s in range(STAGES)]
        s_gamma = sem("gamma_sigmoid")
        s_g_ident = sem("gamma_diagonal")
        s_qk = sem("qk_projected")
        s_qk_copied = sem("qk_copied")
        s_sim = sem("sim_ready")
        s_sim_copied = sem("sim_copied")
        s_searched = sem("thresholds_searched")
        s_flags = sem("flags_summed")
        s_slow = sem("slow_order")
        s_sig = sem("sigmoids_ready")
        s_adj = sem("adjacency_ready")
        s_diag = sem("row_scales_ready")
        s_diag_used = sem("row_scales_used")
        s_x1p = sem("x1_summed")
        s_x1 = sem("x1_ready")
        s_x1_stored = sem("x1_stored")
        s_ln2 = sem("ln2_coefs")
        s_h = sem("h_ready")
        s_h_max = sem("h_magnitudes")
        s_h_quant = sem("h_quantised")
        s_hT = sem("h_transposed")
        s_hT_copied = sem("h_transpose_copied")
        s_logits = sem("logits_ready")
        s_rmax = sem("router_shifted")
        s_exp = sem("router_exponentials")
        s_choice = sem("choices_ready")
        s_rank = sem("ranks_ready")
        s_slots = sem("slots_ready")
        s_scattered = [sem(f"first_choices_scattered{u}") for u in range(2)]
        s_second = sem("second_weights_written")
        s_scattered2 = sem("second_choices_scattered")
        s_abs = sem("abs_sums")
        s_wsum = sem("weight_sums")
        s_wscale = sem("weight_scales")
        s_w8 = [sem(f"weights_rounded{s}") for s in range(STAGES)]
        s_zeroed = sem("routed_rows_zeroed")
        s_tables = sem("tile_tables")
        s_xq_free = sem("quantised_rows_left")
        s_clipped = sem("weights_clipped")
        s_expanded = sem("experts_expanded")
        s_xr_in = [sem(f"routed_rows_in{s}") for s in range(2)]
        s_xt = sem("routed_transposed")
        s_xt_copied = sem("routed_transpose_copied")
        s_gu = sem("gate_up_halves")
        s_sq = sem("relu_squared_halves")
        s_act = sem("activated_halves")
        s_aq = sem("activated_quantised")
        s_at = sem("activated_transposed")
        s_at_copied = sem("activated_transpose_copied")
        s_y = sem("down_done")
        s_osc = sem("out_scales")
        s_y_copied = sem("expert_rows_ready")
        s_tokens = sem("tile_tokens_ready")
        s_due = sem("addition_due")
        s_y_free = sem("expert_rows_left")
        s_added = sem("expert_rows_added")
        s_fill = sem("fill_rows_made")

        dve_starts = [s_wscale, s_h_quant, s_h_quant]
        act_starts = [s_abs, s_sim_copied, s_sim_copied] + RT * [s_x1] + [s_hT_copied,
                      s_hT_copied, s_y_copied, s_y_copied]
        pool_starts = [s_y_free, s_y_free]
        pe_starts = [s_wsum, s_logits, s_logits, s_y]
        W_ADJ = STAGES * (COUNTS - 1)
        W_REST = W_ADJ + 2 * B
        assert W_REST == NW - 4
        passing = [(k, k % STAGES) for k in range(W_ADJ)] + [(W_ADJ, 0), (W_ADJ + 1, 1), (W_REST, 2)] + \
                  [(k, (k - W_ADJ) % 2) for k in range(W_ADJ + 2, W_REST)] + \
                  [(W_REST + 1, 0), (W_REST + 2, 1), (W_REST + 3, 2)]
        ADJ_TURN = W_ADJ // STAGES
        LAST_TURN = [sum(1 for _k, s in passing if s == u) for u in range(STAGES)]
        POOL_CLIPS = list(range(W_ADJ)) + list(range(W_ADJ, W_REST, 2))

        block = ctx.enter_context(nc.Block())

        LOOP_FROM, LOOP_TO = 2, TILES - 1
        assert (LOOP_TO - LOOP_FROM) % 2 == 0
        PAIRS = (LOOP_TO - LOOP_FROM) // 2

        @block.sync
        def _(sp):
            sp.dma_start(wq_sb[:, :], wqT).then_inc(s_const_in, 16)
            sp.dma_start(wk_sb[:, :], wkT).then_inc(s_const_in, 16)
            sp.dma_start(router_sb[:, :, :], routerT).then_inc(s_const_in, 16)
            sp.dma_start(g_raw[:, :], gamma.to_broadcast([P, 1])).then_inc(s_const_in, 16)

            def load_weights(n):
                k, s = passing[n]
                e, m = divmod(k, MATS)
                turn = sum(1 for _k, u in passing[:n] if u == s)
                if turn:
                    sp.wait_ge(s_w8[s], turn)
                sp.dma_start(stage[s], weights_dram[m][e]).then_inc(s_w_in[s], 16)

            def load_x(b):
                if b >= 2:
                    sp.wait_ge(s_x_in[b % 2], 16 * (b // 2))
                sp.dma_start(x_all[:, b * RT:(b + 1) * RT, :],
                             x_t[b * RT:(b + 1) * RT].rearrange("t p h -> p t h")).then_inc(s_x_in[b % 2], 16)

            for b in range(B):
                if b >= 2:
                    sp.wait_ge(s_qk, b - 1)
                sp.dma_start(ctx_sb[b % 2], ctxT[b]).then_inc(s_ctx_in[b % 2], 16)
                if b:
                    load_x(b - 1)
            load_weights(0)
            load_x(B - 1)
            for n in range(1, STAGES + 1):
                load_weights(n)
            for n in range(STAGES + 1, NW):
                if n == NW - 1:
                    sp.wait_ge(s_fill, 1)
                    for half in range(2):
                        sp.dma_start(sums[T:T + P, half * (H // 2):(half + 1) * (H // 2)],
                                     fill_rows[:, 0:H // 2]).then_inc(s_zeroed, 16)
                    sp.dma_start(xs[:, :].rearrange("(t p) r -> p t r", p=P),
                                 fill_rows[:, :].unsqueeze(1).to_broadcast([P, TILES, ROW])).then_inc(s_zeroed, 16)
                load_weights(n)

            for u in range(2):
                sp.wait_ge(s_scattered[u], 16 * TT // 2)
            sp.wait_ge(s_scattered2, 16 * TT)

            def load_rows(i, par):
                sp.dma_start(xr_f[par], xs[bass.ds(i * P, P), :]).then_inc(s_xr_in[par], 16)

            load_rows(0, 0)
            load_rows(1, 1)
            with sp.Fori(0, (TILES - 3) // 2) as j:
                for u in range(2):
                    sp.wait_ge(s_xt_copied, 2 * j + u + 1)
                    load_rows(2 * j + u + 2, u)
            assert TILES % 2 == 1
            sp.wait_ge(s_xt_copied, TILES - 2)
            load_rows(TILES - 1, 0)

            sp.wait_ge(s_added, 16 * TILES)

        @block.gpsimd
        def _(pool):
            order = Chain(pool, s_pool_order)
            for s in pool_starts:
                pool.sem_inc(s, 1)
            for m in (ident_f, ident_b):
                order.note(pool.memset(m[:, :], 0.0))
            order.note(pool.memset(tri_b[:, :], 1.0))
            pool.memset(ones_b[:, :], 1.0).then_inc(s_masks, 1)
            pool.memset(ones_f[:, :], 1.0).then_inc(s_masks, 1)
            pool.memset(fill_rows[:, :], 0.0).then_inc(s_masks, 1)
            pool.iota(iota_i[:, 0:E], pattern=[[1, E]], base=0, channel_multiplier=0).then_inc(s_masks, 1)
            pool.iota(iota_i[:, E:E + 1], pattern=[[1, 1]], base=0, channel_multiplier=1).then_inc(s_masks, 1)
            pool.iota(iota_i[:, E + 1:E + 1 + TILES], pattern=[[1, TILES]], base=0, channel_multiplier=0).then_inc(s_masks, 1)
            order.settle()
            for m in (ident_f, ident_b):
                pool.affine_select(out=m[:, :], in_=m[:, :], compare_op=ALU.not_equal, fill=1.0, base=0,
                                   pattern=[[-1, P]], channel_multiplier=1).then_inc(s_masks, 1)
            pool.affine_select(out=tri_b[:, :], in_=tri_b[:, :], compare_op=ALU.is_gt, fill=0.0, base=0,
                               pattern=[[1, P]], channel_multiplier=-1).then_inc(s_masks, 1)

            def clip(k):
                n, s = next((n, s) for n, (m, s) in enumerate(passing) if m == k)
                pool.wait_ge(s_w8[s], 1 + sum(1 for _k, u in passing[:n] if u == s))
                order.note(pool.tensor_scalar(w8[:, k, :], w8[:, k, :], 1.0, -1.0, ALU.min, ALU.max))

            def expand(e):
                order.settle()
                if e:
                    pool.wait_ge(s_expanded, 16 * e)
                o = (e % 2) * MATS * WLEN
                pool.dma_start(slot_w[:, o:o + MATS * WLEN].rearrange("p (m w) -> p m w", m=MATS),
                               w8[:, e * MATS:(e + 1) * MATS, :]).then_inc(s_expanded, 16)

            for k in POOL_CLIPS:
                clip(k)
            pool.wait_ge(s_slots, 1)
            pool.wait_ge(s_zeroed, 48)
            HALF = TT // 2
            for c in range(TOPK):
                for t in range(TT):
                    if c and t % HALF == 0:
                        pool.wait_ge(s_second, t // HALF + 1)
                    pool.indirect_dma_start(
                        xs[:, :], bass.IndirectOffsetOnAxis(ap=slots[:, t, c:c + 1], axis=0),
                        xq_f[:, t, :], None).then_inc(s_scattered2 if c else s_scattered[t // HALF], 16)
                if c == 0:
                    for u in range(2):
                        pool.wait_ge(s_w8[u], LAST_TURN[u])
                    expand(0)
            pool.wait_ge(s_w8[2], LAST_TURN[2])
            pool.wait_ge(s_clipped, B + 1)
            expand(1)

            pool.wait_ge(s_tables, 1)
            pool.wait_ge(s_x1_stored, 16 * B)
            ends_of = [pool.value_load(ends_i[0:1, 0, e:e + 1], min_val=0, max_val=TILES) for e in range(E - 2)]

            def free_slots(tiles_done):
                for e in range(E - 2):
                    with pool.If(ends_of[e] == tiles_done):
                        expand(e + 2)

            def add(i, par):
                if not (isinstance(i, int) and i == 0):
                    pool.wait_ge(s_added, 16 * i)
                    pool.sem_inc(s_y_free, 1)
                pool.wait_ge(s_tokens, i + 1)
                pool.wait_ge(s_y_copied, 2 + i + 1)
                pool.sem_inc(s_due, 1)
                pool.indirect_dma_start(
                    sums[:, :], bass.IndirectOffsetOnAxis(ap=tile_tokens[par][:, :], axis=0),
                    y_sb[par], None, compute_op=ALU.add).then_inc(s_added, 16)
                free_slots(i + 1)

            free_slots(0)
            add(0, 0)
            with pool.Fori(0, (TILES - 1) // 2) as j:
                for u in range(2):
                    add(1 + 2 * j + u, 1 - u)

        @block.tensor
        def _(pe):
            for s in pe_starts:
                pe.sem_inc(s, 1)
            pe.wait_ge(s_const_in, 64)
            pe.wait_ge(s_masks, 9)
            logit_bank, rank_bank = bank[0], bank[1]

            def weight_sum(k, sums, into=bank[7], col=0):
                pe.wait_ge(s_abs, 1 + sums)
                nc.tensor.matmul(into[:, col:col + 1], ones_f[:, :], abs_part[:, bass.ds(k, 1)],
                                 start=True, stop=True).then_inc(s_wsum, 1)

            with pe.Fori(0, B // 2) as b2:
                for u in range(2):
                    b = 2 * b2 + u
                    q_bank, k_bank = bank[2 * u], bank[2 * u + 1]
                    pe.wait_ge(s_ctx_in[u], 16 * b2 + 16)
                    nc.tensor.matmul(q_bank[:, :], wq_sb[:, :], ctx_sb[u], start=True, stop=True)
                    nc.tensor.matmul(k_bank[:, :], wk_sb[:, :], ctx_sb[u], start=True, stop=True).then_inc(s_qk, 1)
                    pe.wait_ge(s_qk_copied, 2 * b + 2)
                    for t in range(RT):
                        pe.wait_ge(s_sim_copied, RT * b + t + 1)
                        nc.tensor.matmul(bank[4 + t % 2][:, :], q_sb[u][:, t * P:(t + 1) * P], k_sb[u],
                                         start=True, stop=True).then_inc(s_sim, 1)
            with pe.Fori(0, COUNTS - 1) as j:
                for m in range(STAGES):
                    pe.wait_ge(s_wscale, 1 + STAGES * j + m)
                    weight_sum(STAGES * j + m, STAGES * j + m + 1)
            pe.wait_ge(s_searched, 1)
            nc.tensor.matmul(bank[6][:, 0:TT], ones_f[:, :], bad[:, :], start=True, stop=True).then_inc(s_flags, 1)
            pe.wait_ge(s_g_ident, 1)

            def x1_sums(b, first=False):
                k = W_ADJ + 2 * b
                pe.wait_ge(s_wscale, 1 + k)
                weight_sum(k, k + (1 if first else 2))
                pe.wait_ge(s_diag, b + 1)
                for i in range(RT):
                    pe.wait_ge(s_x1, RT * b + i + 1)
                    last = nc.tensor.matmul(bank[2 + i][:, :], diag[:, i, :], x_all[:, bass.ds(b * RT + i, 1), :],
                                            start=True, stop=False)
                last.then_inc(s_diag_used, 1)
                weight_sum(k + 1, k + (2 if first else 3), bank[6])
                pe.wait_ge(s_adj, RT * b + RT)
                for i in range(RT):
                    into = bank[2 + i]
                    nc.tensor.matmul(into[:, :], g_ident[:, :], sig[:, i, :], start=False, stop=False)
                    for j in range(RT):
                        last = nc.tensor.matmul(into[:, j * P:(j + 1) * P], sig[:, j, i * P:(i + 1) * P],
                                                g_ident[:, :], start=False, stop=(j == RT - 1))
                    last.then_inc(s_x1p, 1)

            x1_sums(0, first=True)
            with pe.Fori(1, B) as b:
                x1_sums(b)
            pe.wait_ge(s_wscale, 1 + W_REST)
            for m in range(3):
                weight_sum(W_REST + m, W_REST + m + 1, col=m)
            with pe.Fori(0, B // 2) as b2:
                def transposes(b, u, t):
                    into = bank[2 + t % 2]
                    pe.wait_ge(s_h, RT * b + t + 1)
                    pe.wait_ge(s_hT_copied, RT * b + t + 1)
                    for k in range(KH):
                        last = nc.tensor.transpose(into[:, k * P:(k + 1) * P],
                                                   h_sb[u][:, t, k * P:(k + 1) * P], ident_f[:, :])
                    last.then_inc(s_hT, 1)

                def logits(b, t):
                    pe.wait_ge(s_hT_copied, 2 + RT * b + t + 1)
                    for k in range(KH):
                        last = nc.tensor.matmul(logit_bank[:, bass.ds((b * RT + t) * E, E)], hT[t % 2][:, k, :],
                                                router_sb[:, k, :], start=(k == 0), stop=(k == KH - 1))
                    last.then_inc(s_logits, 1)

                for u in range(2):
                    b = 2 * b2 + u
                    transposes(b, u, 0)
                    for t in range(RT):
                        if t < RT - 1:
                            transposes(b, u, t + 1)
                        logits(b, t)
            pe.wait_ge(s_choice, 1)
            rows = TT * E
            nc.tensor.matmul(rank_bank[:, 0:rows], tri_b[:, :], m_b[:, :, :].rearrange("p t e -> p (t e)"),
                             start=True, stop=False)
            for s in range(1, TT):
                nc.tensor.matmul(rank_bank[:, s * E:rows], ones_b[:, :],
                                 m_b[:, 0:TT - s, :].rearrange("p t e -> p (t e)"),
                                 start=False, stop=(s == TT - 1))
            for t in range(TT):
                last = nc.tensor.matmul(rank_bank[:, rows:rows + E], ones_b[:, :], m_b[:, t, :],
                                        start=(t == 0), stop=(t == TT - 1))
            last.then_inc(s_rank, 1)
            weight_sum(NW - 1, NW)

            xT_bank = bank[4][:, 0:H // 2].bitcast(BF16)
            aT_bank = bank[5][:, :].bitcast(BF16)
            pe.wait_ge(s_tables, 1)

            def expert(i):
                return pe.value_load(tab_i[0:1, bass.ds(i, 1)], min_val=0, max_val=E - 1)

            def rows_T(i, par):
                pe.wait_ge(s_xr_in[par], 16 * (i // 2) + 16 if isinstance(i, int) else i * 8 + 16 - 8 * par)
                pe.wait_ge(s_xt_copied, i)
                for k in range(KH):
                    last = nc.tensor.transpose(xT_bank[:, k * P:(k + 1) * P], xr[par][:, k * P:(k + 1) * P],
                                               ident_b[:, :])
                last.then_inc(s_xt, 1)

            def gate_up(i, par):
                e = expert(i)
                at = (e & 1) * (MATS * WLEN)
                pe.wait_ge(s_expanded, e * 16 + 16)
                pe.wait_ge(s_xt_copied, i + 1)
                for hf in range(2):
                    if not (isinstance(i, int) and i == 0):
                        pe.wait_ge(s_act, 2 * i - 1 + hf)
                    for m in range(2):
                        for k in range(KH):
                            last = nc.tensor.matmul(
                                bank[2 * hf + m][:, :], xT[par][:, k, :],
                                slot_w[:, bass.ds(at + (m * WLEN + k * I + hf * 512), 512)],
                                start=(k == 0), stop=(k == KH - 1))
                    last.then_inc(s_gu, 1)

            def act_T(i, par):
                pe.wait_ge(s_aq, i + 1)
                pe.wait_ge(s_at_copied, i)
                for k in range(KI):
                    last = nc.tensor.transpose(aT_bank[:, k * P:(k + 1) * P], aq[par][:, k * P:(k + 1) * P],
                                               ident_b[:, :])
                last.then_inc(s_at, 1)

            def down(i, par):
                e = expert(i)
                at = (e & 1) * (MATS * WLEN)
                pe.wait_ge(s_at_copied, i + 1)
                if not (isinstance(i, int) and i < 2):
                    pe.wait_ge(s_y_copied, 2 + i - 1)
                for k in range(KI):
                    last = nc.tensor.matmul(bank[6 + par][:, :], aT[par][:, k, :],
                                            slot_w[:, bass.ds(at + (2 * WLEN + k * H), H)],
                                            start=(k == 0), stop=(k == KI - 1))
                last.then_inc(s_y, 1)

            rows_T(0, 0)
            rows_T(1, 1)
            gate_up(0, 0)
            rows_T(2, 0)
            gate_up(1, 1)
            act_T(0, 0)
            with pe.Fori(0, PAIRS) as j:
                for u in range(2):
                    i = LOOP_FROM + 2 * j + u
                    rows_T(i + 1, 1 - u)
                    gate_up(i, u)
                    act_T(i - 1, 1 - u)
                    down(i - 2, u)
            i = TILES - 1
            gate_up(i, 0)
            act_T(i - 1, 1)
            down(i - 2, 0)
            act_T(i, 0)
            down(i - 1, 1)
            down(i, 0)

        @block.scalar
        def _(act):
            for s in act_starts:
                act.sem_inc(s, 1)
            act.wait_ge(s_const_in, 64)
            nc.scalar.activation(g_sig[:, :], g_raw[:, :], ACT.Sigmoid).then_inc(s_gamma, 1)

            def magnitude(k, s, turn, sums=None, into=w_junk):
                act.wait_ge(s_w_in[s], 16 * turn + 16)
                act.wait_ge(s_abs, k + 1 if sums is None else sums)
                act.wait_ge(s_gamma, 1)
                nc.scalar.activation(into, stage[s], ACT.Abs,
                                     accum_out=abs_part[:, bass.ds(k, 1)]).then_inc(s_abs, 1)

            def rounded(k, s):
                act.wait_ge(s_wscale, 1 + k + 1)
                act.wait_ge(s_gamma, 1)
                nc.scalar.activation(w8[:, bass.ds(k, 1), :], stage[s], ACT.Copy,
                                     scale=wscale[:, bass.ds(k, 1)]).then_inc(s_w8[s], 1)

            with act.Fori(0, B // 2) as b2:
                for u in range(2):
                    b = 2 * b2 + u
                    act.wait_ge(s_qk, b + 1)
                    nc.scalar.copy(q_sb[u], bank[2 * u][:, :]).then_inc(s_qk_copied, 1)
                    nc.scalar.copy(k_sb[u], bank[2 * u + 1][:, :]).then_inc(s_qk_copied, 1)
                    for t in range(RT):
                        act.wait_ge(s_sim, RT * b + t + 1)
                        act.wait_ge(s_gamma, 1)
                        nc.scalar.mul(sim[:, bass.ds(RT * b + t, 1), :], bank[4 + t % 2][:, :],
                                      SIM_SCALE).then_inc(s_sim_copied, 1)

            def three(k, turn):
                magnitude(k, 0, turn)
                magnitude(k + 1, 1, turn)
                rounded(k, 0)
                magnitude(k + 2, 2, turn)
                rounded(k + 1, 1)

            with act.Fori(0, COUNTS - 1) as j:
                three(STAGES * j, j)
            act.wait_ge(s_searched, 2)

            def x1_out(b):
                for t in range(RT):
                    act.wait_ge(s_x1p, RT * b + t + 1)
                    act.wait_ge(s_gamma, 1)
                    nc.scalar.activation(x_all[:, bass.ds(RT * b + t, 1), :], bank[2 + t][:, :], ACT.Identity,
                                         bias=b1[:, bass.ds(RT * b + t, 1)]).then_inc(s_x1, 1)
                act.wait_ge(s_x1, RT + RT * b + RT)
                act.dma_start(sums[bass.ds(b * N, N), :].rearrange("(t p) h -> p t h", p=P),
                              x_all[:, bass.ds(RT * b, RT), :]).then_inc(s_x1_stored, 16)

            def batch(b, first=False):
                k = W_ADJ + 2 * b
                magnitude(k, 0, ADJ_TURN + b, k + (1 if first else 2))
                if not first:
                    act.wait_ge(s_x1p, RT * b)
                    act.wait_ge(s_gamma, 1)
                for t in range(RT):
                    nc.scalar.activation(sig[:, t, :], sim[:, bass.ds(RT * b + t, 1), :], ACT.Sigmoid).then_inc(s_sig, 1)
                if not first:
                    x1_out(b - 1)
                rounded(k, 0)
                magnitude(k + 1, 1, ADJ_TURN + b, k + (2 if first else 3))
                if first:
                    magnitude(W_REST, 2, ADJ_TURN, k + 3)

            batch(0, first=True)
            with act.Fori(1, B) as b:
                batch(b)
            x1_out(B - 1)
            for m in (1, 2):
                magnitude(W_REST + m, m - 1, ADJ_TURN + B)
            act.wait_ge(s_ln2, 1)
            with act.Fori(0, B // 2) as b2:
                for u in range(2):
                    b = 2 * b2 + u
                    act.wait_ge(s_h_quant, b + 1)
                    act.wait_ge(s_gamma, 1)
                    for t in range(RT):
                        at = bass.ds(RT * b + t, 1)
                        nc.scalar.activation(h_sb[u][:, t, :], x_all[:, at, :], ACT.Identity, bias=b_ln2[:, at],
                                             scale=a_ln2[:, at]).then_inc(s_h, 1)
                    for t in range(RT):
                        act.wait_ge(s_hT, RT * b + t + 1)
                        act.wait_ge(s_logits, RT * b + t + 1)
                        nc.scalar.copy(hT[t % 2].rearrange("p k n -> p (k n)"), bank[2 + t % 2][:, :]).then_inc(s_hT_copied, 1)
            act.wait_ge(s_rmax, 1)
            nc.scalar.activation(rt[:, 2, :, :], rt[:, 1, :, :], ACT.Exp).then_inc(s_exp, 1)
            for m, s in ((1, 0), (2, 1), (0, 2)):
                rounded(W_REST + m, s)
            magnitude(NW - 1, 2, LAST_TURN[2] - 1, into=w8[:, NW - 1, :])
            rounded(NW - 1, 2)

            def squares(i):
                for hf in range(2):
                    act.wait_ge(s_gu, 2 * i + hf + 1)
                    nc.scalar.activation(relu_sb[hf], bank[2 * hf][:, :], ACT.Relu).then_inc(s_act_order, 1)
                    act.wait_ge(s_act_order, 2 * i + hf + 1)
                    if not (isinstance(i, int) and i == 0):
                        act.wait_ge(s_act, 2 * i - 1 + hf)
                    nc.scalar.activation(sq_sb[hf], relu_sb[hf], ACT.Square).then_inc(s_sq, 1)

            def copy_T(i, par):
                act.wait_ge(s_at, i + 1)
                if not (isinstance(i, int) and i < 2):
                    act.wait_ge(s_y, 1 + i - 1)
                nc.scalar.copy(aT[par].rearrange("p k n -> p (k n)"), bank[5][:, :].bitcast(BF16)).then_inc(s_at_copied, 1)

            def scale_y(i, par):
                act.wait_ge(s_y, 1 + i + 1)
                act.wait_ge(s_osc, i + 1)
                act.wait_ge(s_y_free, i + 1)
                act.wait_ge(s_gamma, 1)
                nc.scalar.copy(tile_tokens[par][:, :], tokens[:, bass.ds(i, 1)]).then_inc(s_tokens, 1)
                nc.scalar.activation(y_sb[par], bank[6 + par][:, :], ACT.Copy, scale=osc[par]).then_inc(s_y_copied, 1)

            squares(0)
            squares(1)
            copy_T(0, 0)
            with act.Fori(0, PAIRS) as j:
                for u in range(2):
                    i = LOOP_FROM + 2 * j + u
                    squares(i)
                    copy_T(i - 1, 1 - u)
                    scale_y(i - 2, u)
            i = TILES - 1
            squares(i)
            copy_T(i - 1, 1)
            scale_y(i - 2, 0)
            copy_T(i, 0)
            scale_y(i - 1, 1)
            scale_y(i, 0)

        @block.vector
        def _(dve):
            V = nc.vector
            chain = Chain(dve, s_dve_order)
            for s in dve_starts:
                dve.sem_inc(s, 1)

            dve.wait_ge(s_masks, 9)
            chain.note(V.tensor_copy(iota_e[:, :], iota_i[:, 0:E]))
            chain.note(V.tensor_copy(iota_p[:, :], iota_i[:, E:E + 1]))
            chain.note(V.tensor_copy(iota_t[:, :], iota_i[:, E + 1:E + 1 + TILES]))
            chain.settle()
            dve.wait_ge(s_gamma, 1)
            chain.note(V.tensor_scalar(g_half[:, :], g_sig[:, :], 0.5, None, ALU.mult))
            chain(V.tensor_scalar(g_rest[:, :], g_sig[:, :], -1.0, 1.0, ALU.mult, ALU.add))
            V.tensor_scalar(g_ident[:, :], ident_f[:, :], g_half[:, :], None, ALU.mult).then_inc(s_g_ident, 1)
            V.tensor_scalar(fill_rows[:, TOKEN:TOKEN + 1], iota_p[:, :], float(T), None, ALU.add).then_inc(s_fill, 1)
            chain.note(V.memset(low[:, 1, :], LOW_END[1]))
            chain.note(V.memset(high[:, 1, :], HIGH_END[1]))

            def row(tiles, i):
                return tiles[:, bass.ds(i, 1), :].rearrange("p a n -> p (a n)")

            def apart():
                dve.wait_ge(s_masks, 9)

            def mean_var(g):
                even, odd = st[:, g, :, 1], st[:, g, :, 4]
                total, gap, squares, gap2 = (nw[:, n, g, :] for n in range(4))
                chain.note(V.tensor_tensor(total, even, odd, ALU.add))
                chain.note(V.tensor_tensor(gap, even, odd, ALU.subtract))
                chain(V.tensor_tensor(squares, st[:, g, :, 2], st[:, g, :, 5], ALU.add))
                chain.note(V.tensor_scalar(mean[:, g, :], total, 0.5, None, ALU.mult))
                chain(V.tensor_tensor(gap2, gap, gap, ALU.mult))
                chain(V.scalar_tensor_tensor(gap2, gap2, N / 4.0, squares, ALU.mult, ALU.add))
                chain(V.tensor_scalar(var[:, g, :], gap2, 1.0 / N, None, ALU.mult))

            def inverse_roots(g):
                v, y, t, bits = (nw[:, n, g, :] for n in range(4))
                chain.note(V.tensor_scalar(nw[:, 0, 0, :], var[:, 0, :], EPS, None, ALU.add))
                if g.stop > 1:
                    chain.note(V.tensor_copy(nw[:, 0, 1, :], var[:, 1, :]))
                chain.settle()
                chain(V.tensor_scalar(bits.bitcast(I32), v.bitcast(I32), 1, None, ALU.logical_shift_right))
                chain(V.tensor_scalar(y.bitcast(I32), bits.bitcast(I32), -1.0, float(0x5F3759DF), ALU.mult, ALU.add))
                for r in range(3):
                    chain(V.tensor_tensor(t, y, y, ALU.mult))
                    chain(V.tensor_tensor(t, t, v, ALU.mult))
                    chain(V.tensor_scalar(t, t, -0.5, 1.5, ALU.mult, ALU.add))
                    chain(V.tensor_tensor(rstd[:, g, :] if r == 2 else y, y, t, ALU.mult))

            def weight_scale(k, column=0, sums=None, source=bank[7]):
                col = bass.ds(k, 1)
                dve.wait_ge(s_wsum, 1 + (k + 1 if sums is None else sums))
                apart()
                chain(V.tensor_scalar(wmean[:, col], source[:, column:column + 1], 1.0 / (P * WLEN), EPS,
                                      ALU.mult, ALU.max))
                V.reciprocal(wscale[:, col], wmean[:, col]).then_inc(s_wscale, 1)

            def rounded(k, s):
                dve.wait_ge(s_wscale, 1 + k + 1)
                apart()
                V.tensor_scalar(row(w8, k), stage[s], wscale[:, bass.ds(k, 1)], 1.0,
                                ALU.mult, ALU.min).then_inc(s_w8[s], 1)

            chain.restart()
            with dve.Fori(0, B // 2) as b2:
                for u in range(2):
                    b = 2 * b2 + u
                    for t in range(RT):
                        dve.wait_ge(s_sim_copied, 2 + RT * b + t + 1)
                        apart()
                        chain.note(V.bn_stats(row(st[:, 1], RT * b + t), row(sim, RT * b + t)))
                    dve.wait_ge(s_x_in[u], 16 * b2 + 16)
                    apart()
                    for t in range(RT):
                        chain.note(V.bn_stats(row(st[:, 0], RT * b + t), row(x_all, RT * b + t)))
                chain.restart()
            mean_var(slice(0, 2))
            inverse_roots(slice(0, 2))
            chain.note(V.tensor_scalar(a1[:, :], rstd[:, 0, :], g_rest[:, :], 1.0, ALU.mult, ALU.add))
            chain.note(V.tensor_tensor(nw[:, 0, 0, :], mean[:, 0, :], rstd[:, 0, :], ALU.mult))
            chain(V.tensor_tensor(nw[:, 1, 0, :], var[:, 1, :], rstd[:, 1, :], ALU.mult))
            chain.note(V.tensor_scalar(b1[:, :], nw[:, 0, 0, :], g_rest[:, :], -1.0, ALU.mult, ALU.mult))
            for end_of, (deviations, _above) in ((low, LOW_END), (high, HIGH_END)):
                chain.note(V.scalar_tensor_tensor(end_of[:, 0, :], nw[:, 1, 0, :], deviations, mean[:, 1, :],
                                                  ALU.mult, ALU.add))
            chain.settle()
            chain(V.tensor_copy(now[:, :, :], low[:, :, :]))
            chain.restart()

            def count(beside):
                above, not_above = side[:, 0, :], side[:, 1, :]
                pair = lambda mask: mask.unsqueeze(1).to_broadcast([P, 2, TT])
                chain.note(V.tensor_scalar(above, now[:, 1, :], TARGET, None, ALU.is_gt))
                chain(V.tensor_scalar(not_above, now[:, 1, :], TARGET, None, ALU.is_lt))
                chain.note(V.copy_predicated(low[:, :, :], pair(above), now[:, :, :]))
                chain(V.copy_predicated(high[:, :, :], pair(not_above), now[:, :, :]))
                chain(V.tensor_tensor(span[:, :, :], high[:, :, :], low[:, :, :], ALU.subtract))
                chain.note(V.reciprocal(nw[:, 0, 0, :], span[:, 1, :]))
                chain(V.scalar_tensor_tensor(nw[:, 1, 0, :], low[:, 1, :], TARGET, span[:, 0, :],
                                             ALU.subtract, ALU.mult))
                chain(V.tensor_tensor(nw[:, 2, 0, :], nw[:, 0, 0, :], nw[:, 1, 0, :], ALU.mult))
                chain(V.tensor_tensor(now[:, 0, :], low[:, 0, :], nw[:, 2, 0, :], ALU.subtract))
                marks = []
                for i in range(TT):
                    if i >= RT:
                        chain.after(marks[i - RT])
                    chain.note(V.tensor_scalar(junk[i % RT], sim[:, i, :], now[:, 0, i:i + 1], None,
                                               ALU.is_gt, ALU.add, accum_out=now[:, 1, i:i + 1]))
                    marks.append(chain.n)
                    if i in beside:
                        beside[i]()
                chain.settle()

            with dve.Fori(0, COUNTS - 1) as j:
                k = STAGES * j
                count({TT // 2 - 3: lambda: weight_scale(k), TT - 4: lambda: weight_scale(k + 1),
                       TT - 1: lambda: (weight_scale(k + 2), rounded(k + 2, 2))})
                chain.restart()
            count({})
            chain(V.tensor_scalar(bad[:, :], now[:, 1, :], -TARGET, None, ALU.add))
            chain(V.tensor_tensor(bad[:, :], bad[:, :], bad[:, :], ALU.mult))
            V.tensor_scalar(bad[:, :], bad[:, :], 16.0, None, ALU.is_gt).then_inc(s_searched, 1)
            chain.note(V.tensor_scalar(place[:, :], now[:, 1, :], -1.0, float(KEEP - 1), ALU.mult, ALU.add))
            dve.wait_ge(s_flags, 1)
            chain.note(V.tensor_copy(flags_i[:, 0:TT], bank[6][:, 0:TT]))
            chain(V.tensor_reduce(flags_i[:, TT:TT + 1], bank[6][:, 0:TT], AX.X, ALU.max))
            chain.restart()

            slow = Chain(dve, s_slow)
            any_bad = dve.value_load(flags_i[0:1, TT:TT + 1], min_val=0, max_val=P)
            with dve.If(any_bad > 0):
                with dve.Fori(0, TT) as i:
                    tile_bad = dve.value_load(flags_i[0:1, bass.ds(i, 1)], min_val=0, max_val=P)
                    with dve.If(tile_bad > 0):
                        slow(V.tensor_copy(below[0], row(sim, i)))
                        for n in range(ROUNDS):
                            slow(V.max(m8[:, 0, :], below[0]))
                            if n < ROUNDS - 1:
                                slow(V.match_replace(below[0], m8[:, 0, :], below[0], LOWEST))
                        c = (KEEP - 1) % 8
                        slow(V.tensor_copy(now[:, 0, bass.ds(i, 1)], m8[:, 0, c:c + 1]))
                        slow(V.tensor_scalar(place[:, bass.ds(i, 1)], m8[:, 0, c:c + 1], 0.0, None, ALU.mult))
                        slow.restart()
            V.engine_nop().then_inc(s_searched, 1)

            def clip(k):
                chain(V.tensor_scalar(row(w8, k), row(w8, k), 1.0, -1.0, ALU.min, ALU.max))

            def x1_stats(b):
                for t in range(RT):
                    dve.wait_ge(s_x1, RT + RT * b + t + 1)
                    apart()
                    chain.note(V.bn_stats(row(st[:, 0], RT * b + t), row(x_all, RT * b + t)))

            def batch(b, first=False):
                chain.note(V.tensor_tensor(pick[:, 0], iota_e[:, :].unsqueeze(1).to_broadcast([P, RT, 8]),
                                           place[:, bass.ds(RT * b, RT)].unsqueeze(2).to_broadcast([P, RT, 8]),
                                           ALU.is_equal))
                k = W_ADJ + 2 * b
                for half in range(2):
                    if half:
                        weight_scale(k)
                    marks = []
                    for t in (2 * half, 2 * half + 1):
                        chain.note(V.tensor_scalar(below[t % 2], row(sim, RT * b + t),
                                                   now[:, 0, bass.ds(RT * b + t, 1)], LOWEST, ALU.is_gt, ALU.mult))
                        marks.append(chain.n)
                    for t in (2 * half, 2 * half + 1):
                        chain.after(marks[t % 2])
                        chain.note(V.tensor_tensor(below[t % 2], below[t % 2], row(sim, RT * b + t), ALU.add))
                        marks[t % 2] = chain.n
                    for t in (2 * half, 2 * half + 1):
                        chain.after(marks[t % 2])
                        chain.note(V.max(m8[:, t, :], below[t % 2]))
                    chain.settle()
                chain.note(V.tensor_tensor(pick[:, 1], pick[:, 0], m8[:, :, :], ALU.mult))
                if not first:
                    dve.wait_ge(s_diag_used, b)
                    apart()
                for t in range(RT):
                    chain.note(V.tensor_scalar(diag[:, t, :], ident_f[:, :], a1[:, bass.ds(RT * b + t, 1)], None, ALU.mult))
                chain.settle()
                V.engine_nop().then_inc(s_diag, 1)
                chain(V.tensor_reduce(thr[:, :], pick[:, 1], AX.X, ALU.add))
                for t in range(RT):
                    dve.wait_ge(s_sig, RT * b + t + 1)
                    apart()
                    V.scalar_tensor_tensor(sig[:, t, :], row(sim, RT * b + t), thr[:, t:t + 1], sig[:, t, :],
                                           ALU.is_ge, ALU.mult).then_inc(s_adj, 1)
                weight_scale(k + 1, source=bank[6])
                rounded(k + 1, 1)
                if not first:
                    x1_stats(b - 1)
                dve.wait_ge(s_w8[1], ADJ_TURN + b + 1)
                apart()
                clip(k + 1)
                V.engine_nop().then_inc(s_clipped, 1)
                chain.restart()

            batch(0, first=True)
            with dve.Fori(1, B) as b:
                batch(b)
            x1_stats(B - 1)
            chain.settle()

            mean_var(slice(0, 1))
            inverse_roots(slice(0, 1))
            chain.note(V.tensor_copy(a_ln2[:, :], rstd[:, 0, :]))
            chain(V.scalar_tensor_tensor(b_ln2[:, :], mean[:, 0, :], -1.0, rstd[:, 0, :], ALU.mult, ALU.mult))
            V.engine_nop().then_inc(s_ln2, 1)
            for m in range(3):
                weight_scale(W_REST + m, m, W_REST + 3)
            chain.restart()
            with dve.Fori(0, B // 2) as b2:
                for u in range(2):
                    b = 2 * b2 + u
                    for t in range(RT):
                        dve.wait_ge(s_h, RT * b + t + 1)
                        chain.note(V.tensor_reduce(hm[:, 0, t:t + 1], h_sb[u][:, t, :], AX.X, ALU.max,
                                                   apply_absolute_value=True))
                    chain.settle()
                    chain(V.tensor_scalar(hm[:, 1, :], hm[:, 0, :], EPS, 1.0 / 127.0, ALU.max, ALU.mult))
                    chain.note(V.reciprocal(hm[:, 2, :], hm[:, 1, :]))
                    chain(V.tensor_tensor(hm[:, 3, :], hm[:, 1, :], hm[:, 1, :], ALU.mult))
                    chain.note(V.tensor_tensor(xq_f[:, bass.ds(RT * b, RT), SCALE], hm[:, 3, :], hm[:, 1, :], ALU.mult))
                    marks = []
                    for t in range(RT):
                        dve.wait_ge(s_hT, RT * b + t + 1)
                        chain.note(V.tensor_scalar(h_sb[u][:, t, :], h_sb[u][:, t, :], hm[:, 2, t:t + 1], MAGIC,
                                                   ALU.mult, ALU.add))
                        marks.append(chain.n)
                    for t in range(RT):
                        chain.after(marks[t])
                        chain.note(V.tensor_scalar(row(xq, RT * b + t)[:, 0:H], h_sb[u][:, t, :], MAGIC, 127.0,
                                                   ALU.subtract, ALU.min))
                    chain.settle()
                    V.engine_nop().then_inc(s_h_quant, 1)
                chain.restart()
            dve.wait_ge(s_x1_stored, 16 * B)

            dve.wait_ge(s_logits, 2 + TT)
            flat = lambda n: rt[:, n, :, :].rearrange("p t e -> p (t e)")
            logits = bank[0][:, 0:TT * E].rearrange("p (t e) -> p t e", e=E)
            wide = lambda v: v.unsqueeze(2).to_broadcast([P, TT, E])
            e_wide = iota_e[:, :].unsqueeze(1).to_broadcast([P, TT, E])
            red = small
            chain(V.tensor_reduce(red[:, 0, :], logits, AX.X, ALU.max))
            V.tensor_tensor(rt[:, 1, :, :], logits, wide(red[:, 0, :]), ALU.subtract).then_inc(s_rmax, 1)
            dve.wait_ge(s_exp, 1)
            chain(V.tensor_reduce(red[:, 1, :], rt[:, 2, :, :], AX.X, ALU.add))
            chain(V.reciprocal(red[:, 2, :], red[:, 1, :]))
            chain(V.tensor_tensor(rt[:, 3, :, :], rt[:, 2, :, :], wide(red[:, 2, :]), ALU.mult))
            for c in range(TOPK):
                prob = rt[:, 3 + 4 * c, :, :]
                top = red[:, 3 + c, :]
                chain(V.tensor_reduce(top, prob, AX.X, ALU.max))
                chain(V.tensor_tensor(rt[:, 4 + 4 * c, :, :], prob, wide(top), ALU.is_lt))
                chain(V.tensor_scalar(flat(5 + 4 * c), flat(4 + 4 * c), 100.0, None, ALU.mult))
                chain(V.tensor_tensor(rt[:, 5 + 4 * c, :, :], rt[:, 5 + 4 * c, :, :], e_wide, ALU.add))
                chain(V.tensor_reduce(red[:, 5 + c, :], rt[:, 5 + 4 * c, :, :], AX.X, ALU.min))
                chain(V.tensor_tensor(rt[:, 6 + 4 * c, :, :], wide(red[:, 5 + c, :]), e_wide, ALU.is_equal))
                if c == 0:
                    chain(V.scalar_tensor_tensor(flat(7), flat(6), -2.0, flat(3), ALU.mult, ALU.add))
            V.tensor_tensor(m_b[:, :, :], rt[:, 6, :, :], rt[:, 10, :, :], ALU.add).then_inc(s_choice, 1)
            chain(V.tensor_tensor(red[:, 7, :], red[:, 3, :], red[:, 4, :], ALU.add))
            chain(V.reciprocal(red[:, 2, :], red[:, 7, :]))
            for c in range(TOPK):
                chain.note(V.tensor_tensor(combine[:, :, c], red[:, 3 + c, :], red[:, 2, :], ALU.mult))
            chain.note(V.tensor_scalar(xq_f[:, :, TOKEN], iota_t[:, 0:TT], float(P), iota_p[:, :], ALU.mult, ALU.add))
            chain.settle()
            chain.note(V.tensor_copy(xq_f[:, :, WEIGHT], combine[:, :, 0]))
            dve.wait_ge(s_rank, 1)
            rows, tiles, end = bank[1][:, TT * E:TT * E + E], ends[:, 0, :], ends[:, 2, :]
            chain(V.tensor_scalar(ends_i[:, 1, :], rows, float(P - 1), None, ALU.add))
            chain(V.tensor_scalar(ends_i[:, 0, :], ends_i[:, 1, :], 7, None, ALU.arith_shift_right))
            chain(V.tensor_copy(tiles, ends_i[:, 0, :]))
            chain.note(V.tensor_copy(ends[:, 1, :], tiles))
            chain.note(V.tensor_copy(ends[:, 2, :], tiles))
            chain.settle()
            src, dst = 1, 2
            for step in (1, 2, 4):
                chain.note(V.tensor_copy(ends[:, dst, 0:step], ends[:, src, 0:step]))
                chain(V.tensor_tensor(ends[:, dst, step:E], ends[:, src, step:E], ends[:, src, 0:E - step], ALU.add))
                src, dst = dst, src
            end = ends[:, src, :]
            chain(V.tensor_tensor(first_row[:, :], end, tiles, ALU.subtract))
            chain(V.tensor_scalar(first_row[:, :], first_row[:, :], float(P), None, ALU.mult))
            chain(V.tensor_tensor(rt[:, 11, :, :], bank[1][:, 0:TT * E].rearrange("p (t e) -> p t e", e=E),
                                  first_row[:, :].unsqueeze(1).to_broadcast([P, TT, E]), ALU.add))
            for c in range(TOPK):
                chain.note(V.tensor_tensor(rt[:, 12 + c, :, :], rt[:, 11, :, :], rt[:, 6 + 4 * c, :, :], ALU.mult))
            chain.settle()
            for c in range(TOPK):
                chain.note(V.tensor_reduce(red[:, c, :], rt[:, 12 + c, :, :], AX.X, ALU.add))
            chain.settle()
            for c in range(TOPK):
                chain.note(V.tensor_copy(slots[:, :, c], red[:, c, :]))
            chain.settle()
            V.engine_nop().then_inc(s_slots, 1)
            chain.note(V.tensor_copy(ends_i[:, 0, :], end))
            chain(V.tensor_tensor(past[:, :, :], iota_t[:, :].unsqueeze(2).to_broadcast([P, TILES, E - 1]),
                                  end[:, 0:E - 1].unsqueeze(1).to_broadcast([P, TILES, E - 1]), ALU.is_ge))
            chain(V.tensor_reduce(tab[:, :], past[:, :, :], AX.X, ALU.add))
            chain(V.tensor_copy(tab_i[:, :], tab[:, :]))
            V.engine_nop().then_inc(s_tables, 1)
            weight_scale(NW - 1)
            half = TT // 2
            for u in range(2):
                dve.wait_ge(s_scattered[u], 16 * half)
                V.tensor_copy(xq_f[:, u * half:(u + 1) * half, WEIGHT],
                              combine[:, u * half:(u + 1) * half, 1]).then_inc(s_second, 1)
            for k, s in ((W_REST + 1, 0), (W_REST + 2, 1), (W_REST, 2), (NW - 1, 2)):
                dve.wait_ge(s_w8[s], LAST_TURN[s] - (1 if k == W_REST else 0))
                clip(k)
            V.engine_nop().then_inc(s_clipped, 1)
            dve.wait_ge(s_wscale, 1 + NW)
            wm = wmean[:, :].rearrange("p (e m) -> p m e", m=MATS)
            chain(V.tensor_tensor(expert_c[:, :], wm[:, 0, :], wm[:, 0, :], ALU.mult))
            chain(V.tensor_tensor(expert_c[:, :], expert_c[:, :], wm[:, 1, :], ALU.mult))
            chain(V.tensor_scalar(expert_d[:, :], wm[:, 2, :], 1.0 / 127.0, None, ALU.mult))

            def rows_in(i, par):
                e = dve.value_load(tab_i[0:1, bass.ds(i, 1)], min_val=0, max_val=E - 1)
                dve.wait_ge(s_xt, i + 1)
                if not (isinstance(i, int) and i < 2):
                    dve.wait_ge(s_gu, 2 * i - 2)
                if not (isinstance(i, int) and i < 2):
                    dve.wait_ge(s_osc, i - 1)
                V.tensor_copy(weight[par], xr_f[par][:, WEIGHT:WEIGHT + 1]).then_inc(s_dve_order, 1)
                V.tensor_copy(tokens[:, bass.ds(i, 1)], xr_f[par][:, TOKEN:TOKEN + 1]).then_inc(s_dve_order, 1)
                V.tensor_scalar(fs[par], xr_f[par][:, SCALE:SCALE + 1], expert_c[:, bass.ds(e, 1)], None,
                                ALU.mult).then_inc(s_dve_order, 1)
                V.tensor_copy(xT[par].rearrange("p k n -> p (k n)"), bank[4][:, 0:H // 2].bitcast(BF16)).then_inc(s_xt_copied, 1)

            def products(i):
                for hf in range(2):
                    dve.wait_ge(s_sq, 2 * i + hf + 1)
                    V.tensor_tensor(act_sb[:, hf * 512:(hf + 1) * 512], bank[2 * hf + 1][:, :], sq_sb[hf],
                                    ALU.mult).then_inc(s_act, 1)

            def quantise(i, par):
                e = dve.value_load(tab_i[0:1, bass.ds(i, 1)], min_val=0, max_val=E - 1)
                top, inv, k = tiny[:, 0:1], tiny[:, 1:2], tiny[:, 2:3]
                dve.wait_ge(s_act, 2 * i + 2)
                chain(V.tensor_reduce(top, act_sb, AX.X, ALU.max, apply_absolute_value=True))
                chain(V.tensor_scalar(top, top, fs[par], EPS, ALU.mult, ALU.max))
                chain(V.reciprocal(inv, top))
                chain(V.tensor_scalar(k, inv, fs[par], 127.0, ALU.mult, ALU.mult))
                chain(V.tensor_scalar(act_r, act_sb, k, MAGIC, ALU.mult, ALU.add))
                if not (isinstance(i, int) and i < 2):
                    dve.wait_ge(s_at, i - 1)
                V.tensor_scalar(aq[par], act_r, MAGIC, 127.0, ALU.subtract, ALU.min).then_inc(s_aq, 1)
                if not (isinstance(i, int) and i < 2):
                    dve.wait_ge(s_y_copied, 2 + i - 1)
                V.tensor_scalar(osc[par], top, expert_d[:, bass.ds(e, 1)], weight[par], ALU.mult, ALU.mult).then_inc(s_osc, 1)

            def step(i, par, more=True):
                if more:
                    rows_in(i + 1, 1 - par)
                    chain.n += 3
                products(i)
                quantise(i, par)

            rows_in(0, 0)
            chain.n += 3
            step(0, 0)
            step(1, 1)
            chain.restart()
            with dve.Fori(0, PAIRS) as j:
                for u in range(2):
                    step(LOOP_FROM + 2 * j + u, u)
                chain.restart()
            step(TILES - 1, 0, more=False)


_INS = ["x", "ctxT", "wqT", "wkT", "gamma", "routerT", "gateT", "upT", "downT"]


def kernel(**inputs):
    import numpy as np
    import concourse.bacc as bacc
    from concourse import mybir as mb
    from concourse.bass_utils import run_bass_kernel_spmd

    a = {k: np.asarray(v) for k, v in inputs.items()}
    c = np.ascontiguousarray
    gate, up, down = a["L0_ffn_gate_w"], a["L0_ffn_up_w"], a["L0_ffn_down_w"]
    E, I, H = gate.shape
    p = 128

    def blocks(w):
        e, r, k = w.shape
        return c(w.reshape(e, r, k // p, p).transpose(0, 3, 2, 1))

    arrays = {
        "x": c(a["x"]),
        "ctxT": c(a["ctx_512"].transpose(0, 2, 1)),
        "wqT": c(a["L0_xattn_Wq"].T),
        "wkT": c(a["L0_xattn_Wk"].T),
        "gamma": c(a["L0_xattn_gamma_raw"].reshape(1, 1)),
        "routerT": c(a["L0_ffn_router_w"].reshape(E, H // p, p).transpose(2, 1, 0)),
        "gateT": blocks(gate),
        "upT": blocks(up),
        "downT": blocks(down),
    }
    nc = bacc.Bacc("TRN2", target_bir_lowering=False, num_devices=1)
    feed, args = {}, []
    for name in _INS:
        arr = arrays[name]
        feed[name + "_in"] = arr
        args.append(nc.dram_tensor(name + "_in", arr.shape, mb.dt.from_np(arr.dtype), kind="ExternalInput").ap())
    tokens = a["x"].shape[0] * a["x"].shape[1]
    out = nc.dram_tensor("out", [tokens + p, H], mb.dt.float32, kind="ExternalOutput").ap()
    build(nc, *args, out)
    r = run_bass_kernel_spmd(nc, [feed], core_ids=[0])
    return r.results[0]["out"][:tokens].reshape(a["x"].shape)
```

```python
from contextlib import ExitStack

import concourse.bass as bass
from concourse import mybir
from concourse.alu_op_type import AluOpType as ALU

F32, BF16, I32, I8 = mybir.dt.float32, mybir.dt.bfloat16, mybir.dt.int32, mybir.dt.int8
ACT = mybir.ActivationFunctionType
AX = mybir.AxisListType
P = 128
EPS = 1e-5
MAGIC = 1.5 * 2.0 ** 23
LOWEST = -3.0e38


class Chain:

    def __init__(self, eng, sem):
        self.eng, self.sem, self.n = eng, sem, 0

    def __call__(self, ins):
        self.note(ins)
        self.settle()

    def note(self, ins):
        ins.then_inc(self.sem, 1)
        self.n += 1

    def settle(self):
        self.eng.wait_ge(self.sem, self.n)

    def after(self, mark):
        self.eng.wait_ge(self.sem, mark)

    def restart(self):
        self.settle()
        self.eng.sem_clear(self.sem)
        self.n = 0


def build(nc, x, ctxT, wqT, wkT, gamma, routerT, gateT, upT, downT, out):
    B, N, H = x.shape
    D = wqT.shape[0]
    E = routerT.shape[-1]
    I = gateT.shape[-1]
    RT = N // P
    KH, KI = H // P, I // P
    T = B * N
    TT = T // P
    TOPK = 2
    KEEP = max(1, int(N * 0.3))
    ROUNDS = -(-KEEP // 8)
    LOW_END, HIGH_END = (-0.4, 0.4383 * N), (1.3, 0.1758 * N)
    COUNTS = 5
    TARGET = KEEP - 4.5
    TILES = T * TOPK // P + E - 1
    ROW = H // 2 + 3
    SCALE, TOKEN, WEIGHT = H // 2, H // 2 + 1, H // 2 + 2
    MATS = 3
    WLEN = KH * I
    NW = E * MATS
    STAGES = 3
    ARENA = 13360
    SIM_SCALE = 1.0 / (float((D // 4) ** 0.5) * 4)

    xs = nc.dram_tensor("routed_rows", [TILES * P, ROW], F32)
    sums = out
    x_t = x.rearrange("b (t p) h -> (b t) p h", p=P)
    weights_dram = tuple(w.rearrange("e p k n -> e p (k n)") for w in (gateT, upT, downT))

    ctx = ExitStack()
    with ctx:
        def sb(name, shape, dt=F32):
            return ctx.enter_context(nc.sbuf_tensor(name, shape, dt))

        def sem(name):
            return ctx.enter_context(nc.semaphore(name))

        bank = [ctx.enter_context(nc.psum_tensor(f"bank{i}", [P, 512], F32)) for i in range(8)]

        w8 = sb("w8", [P, NW, WLEN], I8)
        arena_w = sb("arena_w", [P, 2 * MATS * WLEN], BF16)
        arena = sb("arena", [P, ARENA], F32)
        ident_f = sb("ident_f", [P, P])
        ident_b = sb("ident_b", [P, P], BF16)
        tri_b = sb("tri_b", [P, P], BF16)
        ones_b = sb("ones_b", [P, P], BF16)
        ones_f = sb("ones_f", [P, P])
        wq_sb = sb("wq_sb", [P, P])
        wk_sb = sb("wk_sb", [P, P])
        router_sb = sb("router_sb", [P, KH, E])
        g_raw = sb("g_raw", [P, 1])
        g_sig = sb("g_sig", [P, 1])
        g_half = sb("g_half", [P, 1])
        g_rest = sb("g_rest", [P, 1])
        abs_part = sb("abs_part", [P, NW])
        wmean = sb("wmean", [P, NW])
        wscale = sb("wscale", [P, NW])
        iota_i = sb("iota_i", [P, E + 1 + TILES], I32)
        iota_e = sb("iota_e", [P, E])
        iota_p = sb("iota_p", [P, 1])
        iota_t = sb("iota_t", [P, TILES])
        g_ident = sb("g_ident", [P, P])
        first_row = sb("first_row", [P, E])
        slots = sb("slots", [P, TT, TOPK], I32)
        combine = sb("combine", [P, TT, TOPK])
        fill_rows = sb("fill_rows", [P, ROW])
        tile_tokens = [sb(f"tile_tokens{u}", [P, 1], I32) for u in range(2)]
        tab = sb("tab", [P, TILES])
        tab_i = sb("tab_i", [P, TILES], I32)
        parity = sb("parity", [P, TILES], I32)
        pair_words = sb("pair_words", [P, 2, TILES], I32)
        ends = sb("ends", [P, 3, E])
        ends_i = sb("ends_i", [P, 2, E], I32)
        expert_c = sb("expert_c", [P, E])
        expert_d = sb("expert_d", [P, E])
        small = sb("small", [P, 8, TT])
        m_b = sb("m_b", [P, TT, E], BF16)
        st = sb("st", [P, 2, TT, 6])
        mean = sb("mean", [P, 2, TT])
        var = sb("var", [P, 2, TT])
        nw = sb("nw", [P, 4, 2, TT])
        rstd = sb("rstd", [P, 2, TT])
        a1 = sb("a1", [P, TT])
        b1 = sb("b1", [P, TT])
        a_ln2 = sb("a_ln2", [P, TT])
        b_ln2 = sb("b_ln2", [P, TT])
        now = sb("now", [P, 2, TT])
        low = sb("low", [P, 2, TT])
        high = sb("high", [P, 2, TT])
        span = sb("span", [P, 2, TT])
        side = sb("side", [P, 2, TT], I32)
        place = sb("place", [P, TT])
        bad = sb("bad", [P, TT])
        flags_i = sb("flags_i", [P, TT + 1], I32)
        m8 = sb("m8", [P, RT, 8])
        pick = sb("pick", [P, 2, RT, 8])
        thr = sb("thr", [P, RT])
        hm = sb("hm", [P, 4, RT])
        stage = [arena_w[:, 2 * s * WLEN:2 * (s + 1) * WLEN].bitcast(F32) for s in range(STAGES)]
        slot_w = arena_w[:, :]

        used = [0]

        def carve(n):
            o = used[0]
            used[0] += n
            assert used[0] <= ARENA, used[0]
            return arena[:, o:o + n]

        x_all = carve(TT * H).rearrange("p (t h) -> p t h", t=TT)
        scratch = used[0]
        qk_at = used[0]
        q_sb = [carve(N) for _ in range(2)]
        k_sb = [carve(N) for _ in range(2)]
        sig = carve(RT * N).rearrange("p (t n) -> p t n", t=RT)
        ctx_sb = [carve(N) for _ in range(2)]
        junk = [sig[:, t, :] for t in range(RT)]
        w_junk = arena[:, qk_at:qk_at + WLEN // 4].bitcast(I8)
        used[0] = scratch
        xq_f = carve(TT * ROW).rearrange("p (t h) -> p t h", t=TT)
        xq = xq_f.bitcast(BF16)
        hT = [carve(H).rearrange("p (k n) -> p k n", k=KH) for _ in range(2)]
        lT = [wq_sb, wk_sb]
        used[0] = 0
        rt = carve(14 * TT * E).rearrange("p (n t e) -> p n t e", n=14, t=TT)
        h_sb = [w8[:, NW - 4 + 2 * u:NW - 2 + 2 * u, :].rearrange("p k w -> p (k w)").bitcast(F32)
                .rearrange("p (t h) -> p t h", t=RT) for u in range(2)]
        SIM_MATS = TT * N * 4 // WLEN
        sim = w8[:, NW - SIM_MATS:NW, :].rearrange("p k w -> p (k w)").bitcast(F32).rearrange(
            "p (t n) -> p t n", t=TT)
        below = ctx_sb
        diag = k_sb[0].rearrange("p (t n) -> p t n", t=RT)

        used[0] = 0
        xr_f = [carve(ROW) for _ in range(2)]
        xr = [v.bitcast(BF16) for v in xr_f]
        xT = [carve(H // 2).bitcast(BF16).rearrange("p (k n) -> p k n", k=KH) for _ in range(2)]
        relu_sb = [carve(512) for _ in range(2)]
        assert used[0] >= 14 * TT * E
        tile_c = carve(TILES)
        tile_d = carve(TILES)
        past = carve(TILES * E).rearrange("p (t e) -> p t e", e=E)
        payload = carve(TILES * 2).rearrange("p (t w) -> p t w", w=2)
        sq_sb = [carve(512) for _ in range(2)]
        act_sb = carve(I)
        act_r = carve(I)
        aq = [carve(I // 2).bitcast(BF16) for _ in range(2)]
        aT = [carve(I // 2).bitcast(BF16).rearrange("p (k n) -> p k n", k=KI) for _ in range(2)]
        y_sb = [carve(H) for _ in range(2)]
        fs = [carve(1) for _ in range(2)]
        osc = [carve(1) for _ in range(2)]
        tiny = carve(4)

        s_const_in = sem("const_in")
        s_masks = sem("masks_made")
        s_pool_order = sem("pool_order")
        s_dve_order = sem("dve_order")
        s_act_order = sem("act_order")
        s_ctx_in = [sem(f"ctx_in{u}") for u in range(2)]
        s_x_in = [sem(f"x_in{u}") for u in range(2)]
        s_w_in = [sem(f"weights_in{s}") for s in range(STAGES)]
        s_gamma = sem("gamma_sigmoid")
        s_g_ident = sem("gamma_diagonal")
        s_qk = sem("qk_projected")
        s_qk_copied = sem("qk_copied")
        s_sim = sem("sim_ready")
        s_sim_copied = sem("sim_copied")
        s_searched = sem("thresholds_searched")
        s_flags = sem("flags_summed")
        s_slow = sem("slow_order")
        s_sig = sem("sigmoids_ready")
        s_adj = sem("adjacency_ready")
        s_diag = sem("row_scales_ready")
        s_diag_used = sem("row_scales_used")
        s_x1p = sem("x1_summed")
        s_x1 = sem("x1_ready")
        s_x1_stored = sem("x1_stored")
        s_ln2 = sem("ln2_coefs")
        s_h = sem("h_ready")
        s_h_quant = sem("h_quantised")
        s_hT = sem("h_transposed")
        s_hT_copied = sem("h_transpose_copied")
        s_lT = sem("logits_T_ready")
        s_lT_copied = sem("logits_T_copied")
        s_logits = sem("logits_ready")
        s_rmax = sem("router_shifted")
        s_exp = sem("router_exponentials")
        s_choice = sem("choices_ready")
        s_rank = sem("ranks_ready")
        s_slots = sem("slots_ready")
        s_scattered = [sem(f"first_choices_scattered{u}") for u in range(2)]
        s_second = sem("second_weights_written")
        s_scattered2 = sem("second_choices_scattered")
        s_abs = sem("abs_sums")
        s_wsum = sem("weight_sums")
        s_wscale = sem("weight_scales")
        s_w8 = [sem(f"weights_rounded{s}") for s in range(STAGES)]
        s_zeroed = sem("routed_rows_zeroed")
        s_tables = sem("tile_tables")
        s_clipped = sem("weights_clipped")
        s_gate_up_in = sem("experts_gate_up_expanded")
        s_down_in = sem("experts_down_expanded")
        s_xr_in = [sem(f"routed_rows_in{s}") for s in range(2)]
        s_rows_read = sem("routed_rows_scalars_read")
        s_xt = sem("routed_transposed")
        s_xt_copied = sem("routed_transpose_copied")
        s_gu = sem("gate_up_halves")
        s_sq = sem("relu_squared_halves")
        s_act = sem("activated_halves")
        s_aq = sem("activated_quantised")
        s_at = sem("activated_transposed")
        s_at_copied = sem("activated_transpose_copied")
        s_y = sem("down_done")
        s_osc = sem("out_scales")
        s_y_copied = sem("expert_rows_ready")
        s_tokens = sem("tile_tokens_ready")
        s_due = sem("addition_due")
        s_y_free = sem("expert_rows_left")
        s_added = sem("expert_rows_added")
        s_fill = sem("fill_rows_made")

        dve_starts = [s_wscale, s_h_quant, s_h_quant]
        act_starts = [s_abs, s_sim_copied, s_sim_copied] + RT * [s_x1] + [
            s_hT_copied, s_hT_copied, s_lT_copied, s_lT_copied, s_y_copied, s_y_copied]
        pool_starts = [s_y_free, s_y_free]
        pe_starts = [s_wsum, s_logits, s_logits, s_lT, s_lT, s_y]
        W_ADJ = STAGES * (COUNTS - 1)
        W_REST = W_ADJ + 2 * B
        assert W_REST == NW - 4
        passing = [(k, k % STAGES) for k in range(W_ADJ)] + [(W_ADJ, 0), (W_ADJ + 1, 1), (W_REST, 2)] + \
                  [(k, (k - W_ADJ) % 2) for k in range(W_ADJ + 2, W_REST)] + \
                  [(W_REST + 1, 0), (W_REST + 2, 1), (W_REST + 3, 2)]
        ADJ_TURN = W_ADJ // STAGES
        LAST_TURN = [sum(1 for _k, s in passing if s == u) for u in range(STAGES)]
        POOL_CLIPS = list(range(W_ADJ)) + list(range(W_ADJ, W_REST, 2))

        block = ctx.enter_context(nc.Block())

        LOOP_FROM, LOOP_TO = 2, TILES - 1
        assert (LOOP_TO - LOOP_FROM) % 2 == 0
        PAIRS = (LOOP_TO - LOOP_FROM) // 2
        SLOT_A, EXPERT_A, EXPERT_B, SLOT_B = 1, 2, 16, 128
        assert E == 8

        @block.sync
        def _(sp):
            sp.dma_start(wq_sb[:, :], wqT).then_inc(s_const_in, 16)
            sp.dma_start(wk_sb[:, :], wkT).then_inc(s_const_in, 16)
            sp.dma_start(router_sb[:, :, :], routerT).then_inc(s_const_in, 16)
            sp.dma_start(g_raw[:, :], gamma.to_broadcast([P, 1])).then_inc(s_const_in, 16)

            def load_weights(n):
                k, s = passing[n]
                e, m = divmod(k, MATS)
                turn = sum(1 for _k, u in passing[:n] if u == s)
                if turn:
                    sp.wait_ge(s_w8[s], turn)
                sp.dma_start(stage[s], weights_dram[m][e]).then_inc(s_w_in[s], 16)

            def load_x(b):
                if b >= 2:
                    sp.wait_ge(s_x_in[b % 2], 16 * (b // 2))
                sp.dma_start(x_all[:, b * RT:(b + 1) * RT, :],
                             x_t[b * RT:(b + 1) * RT].rearrange("t p h -> p t h")).then_inc(s_x_in[b % 2], 16)

            for b in range(B):
                if b >= 2:
                    sp.wait_ge(s_qk, b - 1)
                sp.dma_start(ctx_sb[b % 2], ctxT[b]).then_inc(s_ctx_in[b % 2], 16)
                if b:
                    load_x(b - 1)
            load_weights(0)
            load_x(B - 1)
            for n in range(1, STAGES + 1):
                load_weights(n)
            for n in range(STAGES + 1, NW):
                if n == NW - 1:
                    sp.wait_ge(s_fill, 1)
                    for half in range(2):
                        sp.dma_start(sums[T:T + P, half * (H // 2):(half + 1) * (H // 2)],
                                     fill_rows[:, 0:H // 2]).then_inc(s_zeroed, 16)
                    sp.dma_start(xs[:, :].rearrange("(t p) r -> p t r", p=P),
                                 fill_rows[:, :].unsqueeze(1).to_broadcast([P, TILES, ROW])).then_inc(s_zeroed, 16)
                load_weights(n)

            for u in range(2):
                sp.wait_ge(s_scattered[u], 16 * TT // 2)
            sp.wait_ge(s_scattered2, 16 * TT)

            def load_rows(i, par):
                sp.dma_start(xr_f[par], xs[bass.ds(i * P, P), :]).then_inc(s_xr_in[par], 16)

            load_rows(0, 0)
            load_rows(1, 1)
            with sp.Fori(0, (TILES - 3) // 2) as j:
                for u in range(2):
                    sp.wait_ge(s_xt, 2 * j + u + 1)
                    sp.wait_ge(s_rows_read, 2 * j + u + 1)
                    load_rows(2 * j + u + 2, u)
            assert TILES % 2 == 1
            sp.wait_ge(s_xt, TILES - 2)
            sp.wait_ge(s_rows_read, TILES - 2)
            load_rows(TILES - 1, 0)

            sp.wait_ge(s_added, 16 * TILES)

        @block.gpsimd
        def _(pool):
            order = Chain(pool, s_pool_order)
            for s in pool_starts:
                pool.sem_inc(s, 1)
            for m in (ident_f, ident_b):
                order.note(pool.memset(m[:, :], 0.0))
            order.note(pool.memset(tri_b[:, :], 1.0))
            pool.memset(ones_b[:, :], 1.0).then_inc(s_masks, 1)
            pool.memset(ones_f[:, :], 1.0).then_inc(s_masks, 1)
            pool.memset(fill_rows[:, :], 0.0).then_inc(s_masks, 1)
            pool.iota(iota_i[:, 0:E], pattern=[[1, E]], base=0, channel_multiplier=0).then_inc(s_masks, 1)
            pool.iota(iota_i[:, E:E + 1], pattern=[[1, 1]], base=0, channel_multiplier=1).then_inc(s_masks, 1)
            pool.iota(iota_i[:, E + 1:E + 1 + TILES], pattern=[[1, TILES]], base=0, channel_multiplier=0).then_inc(s_masks, 1)
            order.settle()
            for m in (ident_f, ident_b):
                pool.affine_select(out=m[:, :], in_=m[:, :], compare_op=ALU.not_equal, fill=1.0, base=0,
                                   pattern=[[-1, P]], channel_multiplier=1).then_inc(s_masks, 1)
            pool.affine_select(out=tri_b[:, :], in_=tri_b[:, :], compare_op=ALU.is_gt, fill=0.0, base=0,
                               pattern=[[1, P]], channel_multiplier=-1).then_inc(s_masks, 1)

            def clip(k):
                n, s = next((n, s) for n, (m, s) in enumerate(passing) if m == k)
                pool.wait_ge(s_w8[s], 1 + sum(1 for _k, u in passing[:n] if u == s))
                order.note(pool.tensor_scalar(w8[:, k, :], w8[:, k, :], 1.0, -1.0, ALU.min, ALU.max))

            def expand(e, m):
                o = ((e % 2) * MATS + m) * WLEN
                pool.dma_start(slot_w[:, o:o + WLEN], w8[:, e * MATS + m, :]).then_inc(
                    s_down_in if m == 2 else s_gate_up_in, 16)

            def expand_gate_up(e):
                if e:
                    pool.wait_ge(s_gate_up_in, 32 * e)
                expand(e, 0)
                expand(e, 1)

            def expand_down(e):
                if e:
                    pool.wait_ge(s_down_in, 16 * e)
                expand(e, 2)

            for k in POOL_CLIPS:
                clip(k)
            for u in range(2):
                pool.wait_ge(s_w8[u], LAST_TURN[u])
            order.settle()
            expand_gate_up(0)
            expand_down(0)
            pool.wait_ge(s_slots, 1)
            pool.wait_ge(s_zeroed, 48)
            HALF = TT // 2
            for c in range(TOPK):
                for t in range(TT):
                    if c and t % HALF == 0:
                        pool.wait_ge(s_second, t // HALF + 1)
                    pool.indirect_dma_start(
                        xs[:, :], bass.IndirectOffsetOnAxis(ap=slots[:, t, c:c + 1], axis=0),
                        xq_f[:, t, :], None).then_inc(s_scattered2 if c else s_scattered[t // HALF], 16)
            pool.wait_ge(s_xt, 1)
            pool.wait_ge(s_w8[2], LAST_TURN[2])
            pool.wait_ge(s_clipped, 1)
            expand_gate_up(1)
            expand_down(1)

            pool.wait_ge(s_tables, 1)
            pool.wait_ge(s_x1_stored, 16 * B)
            ends_of = [pool.value_load(ends_i[0:1, 0, e:e + 1], min_val=0, max_val=TILES) for e in range(E - 2)]

            def when_ended(tile, expand_next):
                for e in range(E - 2):
                    with pool.If(ends_of[e] == tile):
                        expand_next(e + 2)

            def add(i, par):
                if not (isinstance(i, int) and i == 0):
                    pool.wait_ge(s_added, 16 * i)
                    pool.sem_inc(s_y_free, 1)
                pool.wait_ge(s_tokens, i + 1)
                pool.wait_ge(s_y_copied, 2 + i + 1)
                pool.sem_inc(s_due, 1)
                pool.indirect_dma_start(
                    sums[:, :], bass.IndirectOffsetOnAxis(ap=tile_tokens[par][:, :], axis=0),
                    y_sb[par], None, compute_op=ALU.add).then_inc(s_added, 16)
                for ended in ((1, 2, 3) if isinstance(i, int) and i == 0 else (i + 3,)):
                    when_ended(ended, expand_gate_up)
                when_ended(i + 1, expand_down)

            when_ended(0, expand_gate_up)
            when_ended(0, expand_down)
            add(0, 0)
            with pool.Fori(0, (TILES - 1) // 2) as j:
                for u in range(2):
                    add(1 + 2 * j + u, 1 - u)

        @block.tensor
        def _(pe):
            for s in pe_starts:
                pe.sem_inc(s, 1)
            pe.wait_ge(s_const_in, 64)
            pe.wait_ge(s_masks, 9)
            logit_bank, rank_bank = bank[0], bank[1]

            def weight_sum(k, sums, into=bank[7], col=0):
                pe.wait_ge(s_abs, 1 + sums)
                nc.tensor.matmul(into[:, col:col + 1], ones_f[:, :], abs_part[:, bass.ds(k, 1)],
                                 start=True, stop=True).then_inc(s_wsum, 1)

            with pe.Fori(0, B // 2) as b2:
                for u in range(2):
                    q_bank, k_bank = bank[2 * u], bank[2 * u + 1]
                    pe.wait_ge(s_ctx_in[u], 16 * b2 + 16)
                    nc.tensor.matmul(q_bank[:, :], wq_sb[:, :], ctx_sb[u], start=True, stop=True)
                    nc.tensor.matmul(k_bank[:, :], wk_sb[:, :], ctx_sb[u], start=True, stop=True).then_inc(s_qk, 1)
                for u in range(2):
                    b = 2 * b2 + u
                    pe.wait_ge(s_qk_copied, 2 * b + 2)
                    for t in range(RT):
                        pe.wait_ge(s_sim_copied, RT * b + t + 1)
                        nc.tensor.matmul(bank[4 + t % 2][:, :], q_sb[u][:, t * P:(t + 1) * P], k_sb[u],
                                         start=True, stop=True).then_inc(s_sim, 1)
            with pe.Fori(0, COUNTS - 1) as j:
                for m in range(STAGES):
                    pe.wait_ge(s_wscale, 1 + STAGES * j + m)
                    weight_sum(STAGES * j + m, STAGES * j + m + 1)
            pe.wait_ge(s_searched, 1)
            nc.tensor.matmul(bank[6][:, 0:TT], ones_f[:, :], bad[:, :], start=True, stop=True).then_inc(s_flags, 1)
            pe.wait_ge(s_g_ident, 1)

            def x1_sums(b, first=False):
                k = W_ADJ + 2 * b
                pe.wait_ge(s_wscale, 1 + k)
                weight_sum(k, k + (1 if first else 2))
                pe.wait_ge(s_diag, b + 1)
                for i in range(RT):
                    pe.wait_ge(s_x1, RT * b + i + 1)
                    last = nc.tensor.matmul(bank[2 + i][:, :], diag[:, i, :], x_all[:, bass.ds(b * RT + i, 1), :],
                                            start=True, stop=False)
                last.then_inc(s_diag_used, 1)
                weight_sum(k + 1, k + (2 if first else 3), bank[6])
                pe.wait_ge(s_adj, RT * b + RT)
                for i in range(RT):
                    into = bank[2 + i]
                    nc.tensor.matmul(into[:, :], g_ident[:, :], sig[:, i, :], start=False, stop=False)
                    for j in range(RT):
                        last = nc.tensor.matmul(into[:, j * P:(j + 1) * P], sig[:, j, i * P:(i + 1) * P],
                                                g_ident[:, :], start=False, stop=(j == RT - 1))
                    last.then_inc(s_x1p, 1)

            x1_sums(0, first=True)
            with pe.Fori(1, B) as b:
                x1_sums(b)
            pe.wait_ge(s_wscale, 1 + W_REST)
            for m in range(3):
                weight_sum(W_REST + m, W_REST + m + 1, col=m)
            with pe.Fori(0, B // 2) as b2:
                def transposes(b, u, t):
                    into = bank[2 + t % 2]
                    pe.wait_ge(s_h, RT * b + t + 1)
                    pe.wait_ge(s_hT_copied, RT * b + t + 1)
                    for k in range(KH):
                        last = nc.tensor.transpose(into[:, k * P:(k + 1) * P],
                                                   h_sb[u][:, t, k * P:(k + 1) * P], ident_f[:, :])
                    last.then_inc(s_hT, 1)

                def logits_T(b, t):
                    into = bank[4 + t % 2][0:E, 0:P]
                    pe.wait_ge(s_hT_copied, 2 + RT * b + t + 1)
                    pe.wait_ge(s_lT_copied, RT * b + t + 1)
                    for k in range(KH):
                        last = nc.tensor.matmul(into, router_sb[:, k, :], hT[t % 2][:, k, :],
                                                start=(k == 0), stop=(k == KH - 1))
                    last.then_inc(s_lT, 1)

                def logits(b, t):
                    pe.wait_ge(s_lT_copied, 2 + RT * b + t + 1)
                    nc.tensor.matmul(logit_bank[:, bass.ds((b * RT + t) * E, E)], lT[t % 2][0:E, :],
                                     ident_f[0:E, 0:E], start=True, stop=True).then_inc(s_logits, 1)

                for u in range(2):
                    b = 2 * b2 + u
                    transposes(b, u, 0)
                    for t in range(RT):
                        if t < RT - 1:
                            transposes(b, u, t + 1)
                        logits_T(b, t)
                        if t:
                            logits(b, t - 1)
                    logits(b, RT - 1)
            pe.wait_ge(s_choice, 1)
            rows = TT * E
            nc.tensor.matmul(rank_bank[:, 0:rows], tri_b[:, :], m_b[:, :, :].rearrange("p t e -> p (t e)"),
                             start=True, stop=False)
            for s in range(1, TT):
                nc.tensor.matmul(rank_bank[:, s * E:rows], ones_b[:, :],
                                 m_b[:, 0:TT - s, :].rearrange("p t e -> p (t e)"),
                                 start=False, stop=(s == TT - 1))
            for t in range(TT):
                last = nc.tensor.matmul(rank_bank[:, rows:rows + E], ones_b[:, :], m_b[:, t, :],
                                        start=(t == 0), stop=(t == TT - 1))
            last.then_inc(s_rank, 1)
            weight_sum(NW - 1, NW)

            xT_bank = bank[4][:, 0:H // 2].bitcast(BF16)
            aT_bank = bank[5][:, :].bitcast(BF16)
            pe.wait_ge(s_tables, 1)

            def expert(i):
                return pe.value_load(tab_i[0:1, bass.ds(i, 1)], min_val=0, max_val=E - 1)

            def rows_T(i, par):
                pe.wait_ge(s_xr_in[par], 16 * (i // 2) + 16 if isinstance(i, int) else i * 8 + 16 - 8 * par)
                pe.wait_ge(s_xt_copied, i)
                for k in range(KH):
                    last = nc.tensor.transpose(xT_bank[:, k * P:(k + 1) * P], xr[par][:, k * P:(k + 1) * P],
                                               ident_b[:, :])
                last.then_inc(s_xt, 1)

            def gate_up(i, par, e, unit=1):
                at = (e & unit) * (MATS * WLEN // unit)
                pe.wait_ge(s_gate_up_in, e * (32 // unit) + 32)
                pe.wait_ge(s_down_in, e * (16 // unit) + 16)
                pe.wait_ge(s_xt_copied, i + 1)
                for hf in range(2):
                    if not (isinstance(i, int) and i == 0):
                        pe.wait_ge(s_act, 2 * i - 1 + hf)
                    for m in range(2):
                        for k in range(KH):
                            last = nc.tensor.matmul(
                                bank[2 * hf + m][:, :], xT[par][:, k, :],
                                slot_w[:, bass.ds(at + (m * WLEN + k * I + hf * 512), 512)],
                                start=(k == 0), stop=(k == KH - 1))
                    last.then_inc(s_gu, 1)

            def act_T(i, par):
                pe.wait_ge(s_aq, i + 1)
                pe.wait_ge(s_at_copied, i)
                for k in range(KI):
                    last = nc.tensor.transpose(aT_bank[:, k * P:(k + 1) * P], aq[par][:, k * P:(k + 1) * P],
                                               ident_b[:, :])
                last.then_inc(s_at, 1)

            def down(i, par, e, unit=1):
                at = (e & unit) * (MATS * WLEN // unit)
                pe.wait_ge(s_at_copied, i + 1)
                if not (isinstance(i, int) and i < 2):
                    pe.wait_ge(s_y_copied, 2 + i - 1)
                for k in range(KI):
                    last = nc.tensor.matmul(bank[6 + par][:, :], aT[par][:, k, :],
                                            slot_w[:, bass.ds(at + (2 * WLEN + k * H), H)],
                                            start=(k == 0), stop=(k == KI - 1))
                last.then_inc(s_y, 1)

            rows_T(0, 0)
            rows_T(1, 1)
            gate_up(0, 0, expert(0))
            rows_T(2, 0)
            gate_up(1, 1, expert(1))
            act_T(0, 0)
            with pe.Fori(0, PAIRS) as j:
                word = pe.value_load(pair_words[0:1, 0, bass.ds(j, 1)], min_val=0, max_val=2 * SLOT_B - 1)
                for u, (e_unit, slot_unit) in enumerate(((EXPERT_A, SLOT_A), (EXPERT_B, SLOT_B))):
                    i = LOOP_FROM + 2 * j + u
                    rows_T(i + 1, 1 - u)
                    gate_up(i, u, word & ((E - 1) * e_unit), e_unit)
                    act_T(i - 1, 1 - u)
                    down(i - 2, u, word, slot_unit)
            i = TILES - 1
            gate_up(i, 0, expert(i))
            act_T(i - 1, 1)
            down(i - 2, 0, expert(i - 2))
            act_T(i, 0)
            down(i - 1, 1, expert(i - 1))
            down(i, 0, expert(i))

        @block.scalar
        def _(act):
            for s in act_starts:
                act.sem_inc(s, 1)
            act.wait_ge(s_const_in, 64)
            nc.scalar.activation(g_sig[:, :], g_raw[:, :], ACT.Sigmoid).then_inc(s_gamma, 1)

            def magnitude(k, s, turn, sums=None, into=w_junk):
                act.wait_ge(s_w_in[s], 16 * turn + 16)
                act.wait_ge(s_abs, k + 1 if sums is None else sums)
                act.wait_ge(s_gamma, 1)
                nc.scalar.activation(into, stage[s], ACT.Abs,
                                     accum_out=abs_part[:, bass.ds(k, 1)]).then_inc(s_abs, 1)

            def rounded(k, s):
                act.wait_ge(s_wscale, 1 + k + 1)
                act.wait_ge(s_gamma, 1)
                nc.scalar.activation(w8[:, bass.ds(k, 1), :], stage[s], ACT.Copy,
                                     scale=wscale[:, bass.ds(k, 1)]).then_inc(s_w8[s], 1)

            with act.Fori(0, B // 2) as b2:
                for u in range(2):
                    act.wait_ge(s_qk, 2 * b2 + u + 1)
                    nc.scalar.copy(q_sb[u], bank[2 * u][:, :]).then_inc(s_qk_copied, 1)
                    nc.scalar.copy(k_sb[u], bank[2 * u + 1][:, :]).then_inc(s_qk_copied, 1)
                for u in range(2):
                    b = 2 * b2 + u
                    for t in range(RT):
                        act.wait_ge(s_sim, RT * b + t + 1)
                        act.wait_ge(s_gamma, 1)
                        nc.scalar.mul(sim[:, bass.ds(RT * b + t, 1), :], bank[4 + t % 2][:, :],
                                      SIM_SCALE).then_inc(s_sim_copied, 1)

            def three(k, turn):
                magnitude(k, 0, turn)
                magnitude(k + 1, 1, turn)
                rounded(k, 0)
                magnitude(k + 2, 2, turn)

            with act.Fori(0, COUNTS - 1) as j:
                three(STAGES * j, j)

            def x1_out(b):
                for t in range(RT):
                    act.wait_ge(s_x1p, RT * b + t + 1)
                    act.wait_ge(s_gamma, 1)
                    nc.scalar.activation(x_all[:, bass.ds(RT * b + t, 1), :], bank[2 + t][:, :], ACT.Identity,
                                         bias=b1[:, bass.ds(RT * b + t, 1)]).then_inc(s_x1, 1)
                act.wait_ge(s_x1, RT + RT * b + RT)
                act.dma_start(sums[bass.ds(b * N, N), :].rearrange("(t p) h -> p t h", p=P),
                              x_all[:, bass.ds(RT * b, RT), :]).then_inc(s_x1_stored, 16)

            def batch(b, first=False):
                k = W_ADJ + 2 * b
                magnitude(k, 0, ADJ_TURN + b, k + (1 if first else 2))
                if first:
                    magnitude(k + 1, 1, ADJ_TURN, k + 2)
                    magnitude(W_REST, 2, ADJ_TURN, k + 3)
                    act.wait_ge(s_searched, 2)
                else:
                    act.wait_ge(s_x1p, RT * b)
                    act.wait_ge(s_gamma, 1)
                for t in range(RT):
                    nc.scalar.activation(sig[:, t, :], sim[:, bass.ds(RT * b + t, 1), :], ACT.Sigmoid).then_inc(s_sig, 1)
                if not first:
                    x1_out(b - 1)
                rounded(k, 0)
                if not first:
                    magnitude(k + 1, 1, ADJ_TURN + b, k + 3)

            batch(0, first=True)
            with act.Fori(1, B) as b:
                batch(b)
            x1_out(B - 1)
            for m in (1, 2):
                magnitude(W_REST + m, m - 1, ADJ_TURN + B)
            act.wait_ge(s_ln2, 1)

            def normalised(b, u):
                act.wait_ge(s_h_quant, b + 1)
                act.wait_ge(s_gamma, 1)
                for t in range(RT):
                    at = bass.ds(RT * b + t, 1)
                    nc.scalar.activation(h_sb[u][:, t, :], x_all[:, at, :], ACT.Identity, bias=b_ln2[:, at],
                                         scale=a_ln2[:, at]).then_inc(s_h, 1)

            def copy_hT(b, t):
                act.wait_ge(s_hT, RT * b + t + 1)
                act.wait_ge(s_lT, RT * b + t + 1)
                nc.scalar.copy(hT[t % 2].rearrange("p k n -> p (k n)"), bank[2 + t % 2][:, :]).then_inc(s_hT_copied, 1)

            def copy_lT(b, t):
                act.wait_ge(s_lT, 2 + RT * b + t + 1)
                act.wait_ge(s_logits, RT * b + t + 1)
                nc.scalar.copy(lT[t % 2][0:E, :], bank[4 + t % 2][0:E, 0:P]).then_inc(s_lT_copied, 1)

            def transposed(b):
                copy_hT(b, 0)
                for t in range(RT):
                    if t < RT - 1:
                        copy_hT(b, t + 1)
                    copy_lT(b, t)

            normalised(0, 0)
            with act.Fori(0, B // 2 - 1) as b2:
                for u in range(2):
                    normalised(2 * b2 + u + 1, 1 - u)
                    transposed(2 * b2 + u)
            normalised(B - 1, 1)
            transposed(B - 2)
            transposed(B - 1)
            act.wait_ge(s_rmax, 1)
            nc.scalar.activation(rt[:, 2, :, :], rt[:, 1, :, :], ACT.Exp).then_inc(s_exp, 1)
            for m, s in ((1, 0), (2, 1), (0, 2)):
                rounded(W_REST + m, s)
            magnitude(NW - 1, 2, LAST_TURN[2] - 1, into=w8[:, NW - 1, :])
            rounded(NW - 1, 2)

            def squares(i):
                for hf in range(2):
                    act.wait_ge(s_gu, 2 * i + hf + 1)
                    nc.scalar.activation(relu_sb[hf], bank[2 * hf][:, :], ACT.Relu).then_inc(s_act_order, 1)
                    act.wait_ge(s_act_order, 2 * i + hf + 1)
                    if not (isinstance(i, int) and i == 0):
                        act.wait_ge(s_act, 2 * i - 1 + hf)
                    nc.scalar.activation(sq_sb[hf], relu_sb[hf], ACT.Square).then_inc(s_sq, 1)

            def copy_T(i, par):
                act.wait_ge(s_at, i + 1)
                if not (isinstance(i, int) and i < 2):
                    act.wait_ge(s_y, 1 + i - 1)
                nc.scalar.copy(aT[par].rearrange("p k n -> p (k n)"), bank[5][:, :].bitcast(BF16)).then_inc(s_at_copied, 1)

            def scale_y(i, par):
                act.wait_ge(s_y, 1 + i + 1)
                act.wait_ge(s_osc, i + 1)
                act.wait_ge(s_y_free, i + 1)
                act.wait_ge(s_gamma, 1)
                nc.scalar.copy(tile_tokens[par][:, :], payload[:, bass.ds(i, 1), 0]).then_inc(s_tokens, 1)
                nc.scalar.activation(y_sb[par], bank[6 + par][:, :], ACT.Copy, scale=osc[par]).then_inc(s_y_copied, 1)

            def copy_xT(i, par):
                act.wait_ge(s_xt, i + 1)
                if not (isinstance(i, int) and i < 2):
                    act.wait_ge(s_gu, 2 * i - 2)
                nc.scalar.copy(xT[par].rearrange("p k n -> p (k n)"), bank[4][:, 0:H // 2].bitcast(BF16)).then_inc(s_xt_copied, 1)

            copy_xT(0, 0)
            copy_xT(1, 1)
            squares(0)
            copy_xT(2, 0)
            squares(1)
            copy_T(0, 0)
            with act.Fori(0, PAIRS) as j:
                for u in range(2):
                    i = LOOP_FROM + 2 * j + u
                    copy_xT(i + 1, 1 - u)
                    squares(i)
                    copy_T(i - 1, 1 - u)
                    scale_y(i - 2, u)
            i = TILES - 1
            squares(i)
            copy_T(i - 1, 1)
            scale_y(i - 2, 0)
            copy_T(i, 0)
            scale_y(i - 1, 1)
            scale_y(i, 0)

        @block.vector
        def _(dve):
            V = nc.vector
            chain = Chain(dve, s_dve_order)
            for s in dve_starts:
                dve.sem_inc(s, 1)

            dve.wait_ge(s_masks, 9)
            chain.note(V.tensor_copy(iota_e[:, :], iota_i[:, 0:E]))
            chain.note(V.tensor_copy(iota_p[:, :], iota_i[:, E:E + 1]))
            chain.note(V.tensor_copy(iota_t[:, :], iota_i[:, E + 1:E + 1 + TILES]))
            chain.settle()
            dve.wait_ge(s_gamma, 1)
            chain.note(V.tensor_scalar(g_half[:, :], g_sig[:, :], 0.5, None, ALU.mult))
            chain(V.tensor_scalar(g_rest[:, :], g_sig[:, :], -1.0, 1.0, ALU.mult, ALU.add))
            V.tensor_scalar(g_ident[:, :], ident_f[:, :], g_half[:, :], None, ALU.mult).then_inc(s_g_ident, 1)
            V.tensor_scalar(fill_rows[:, TOKEN:TOKEN + 1], iota_p[:, :], float(T), None, ALU.add).then_inc(s_fill, 1)
            chain.note(V.memset(low[:, 1, :], LOW_END[1]))
            chain.note(V.memset(high[:, 1, :], HIGH_END[1]))

            def row(tiles, i):
                return tiles[:, bass.ds(i, 1), :].rearrange("p a n -> p (a n)")

            def apart():
                dve.wait_ge(s_masks, 9)

            def mean_var(g):
                even, odd = st[:, g, :, 1], st[:, g, :, 4]
                total, gap, squares, gap2 = (nw[:, n, g, :] for n in range(4))
                chain.note(V.tensor_tensor(total, even, odd, ALU.add))
                chain.note(V.tensor_tensor(gap, even, odd, ALU.subtract))
                chain(V.tensor_tensor(squares, st[:, g, :, 2], st[:, g, :, 5], ALU.add))
                chain.note(V.tensor_scalar(mean[:, g, :], total, 0.5, None, ALU.mult))
                chain(V.tensor_tensor(gap2, gap, gap, ALU.mult))
                chain(V.scalar_tensor_tensor(gap2, gap2, N / 4.0, squares, ALU.mult, ALU.add))
                chain(V.tensor_scalar(var[:, g, :], gap2, 1.0 / N, None, ALU.mult))

            def inverse_roots(g):
                v, y, t, bits = (nw[:, n, g, :] for n in range(4))
                chain.note(V.tensor_scalar(nw[:, 0, 0, :], var[:, 0, :], EPS, None, ALU.add))
                if g.stop > 1:
                    chain.note(V.tensor_copy(nw[:, 0, 1, :], var[:, 1, :]))
                chain.settle()
                chain(V.tensor_scalar(bits.bitcast(I32), v.bitcast(I32), 1, None, ALU.logical_shift_right))
                chain(V.tensor_scalar(y.bitcast(I32), bits.bitcast(I32), -1.0, float(0x5F3759DF), ALU.mult, ALU.add))
                for r in range(3):
                    chain(V.tensor_tensor(t, y, y, ALU.mult))
                    chain(V.tensor_tensor(t, t, v, ALU.mult))
                    chain(V.tensor_scalar(t, t, -0.5, 1.5, ALU.mult, ALU.add))
                    chain(V.tensor_tensor(rstd[:, g, :] if r == 2 else y, y, t, ALU.mult))

            def weight_scale(k, column=0, sums=None, source=bank[7]):
                col = bass.ds(k, 1)
                dve.wait_ge(s_wsum, 1 + (k + 1 if sums is None else sums))
                apart()
                chain(V.tensor_scalar(wmean[:, col], source[:, column:column + 1], 1.0 / (P * WLEN), EPS,
                                      ALU.mult, ALU.max))
                V.reciprocal(wscale[:, col], wmean[:, col]).then_inc(s_wscale, 1)

            def rounded(k, s):
                dve.wait_ge(s_wscale, 1 + k + 1)
                apart()
                V.tensor_scalar(row(w8, k), stage[s], wscale[:, bass.ds(k, 1)], 1.0,
                                ALU.mult, ALU.min).then_inc(s_w8[s], 1)

            chain.restart()
            with dve.Fori(0, B // 2) as b2:
                for u in range(2):
                    b = 2 * b2 + u
                    for t in range(RT):
                        dve.wait_ge(s_sim_copied, 2 + RT * b + t + 1)
                        apart()
                        chain.note(V.bn_stats(row(st[:, 1], RT * b + t), row(sim, RT * b + t)))
                    dve.wait_ge(s_x_in[u], 16 * b2 + 16)
                    apart()
                    for t in range(RT):
                        chain.note(V.bn_stats(row(st[:, 0], RT * b + t), row(x_all, RT * b + t)))
                chain.restart()
            mean_var(slice(0, 2))
            inverse_roots(slice(0, 2))
            chain.note(V.tensor_scalar(a1[:, :], rstd[:, 0, :], g_rest[:, :], 1.0, ALU.mult, ALU.add))
            chain.note(V.tensor_tensor(nw[:, 0, 0, :], mean[:, 0, :], rstd[:, 0, :], ALU.mult))
            chain(V.tensor_tensor(nw[:, 1, 0, :], var[:, 1, :], rstd[:, 1, :], ALU.mult))
            chain.note(V.tensor_scalar(b1[:, :], nw[:, 0, 0, :], g_rest[:, :], -1.0, ALU.mult, ALU.mult))
            for end_of, (deviations, _above) in ((low, LOW_END), (high, HIGH_END)):
                chain.note(V.scalar_tensor_tensor(end_of[:, 0, :], nw[:, 1, 0, :], deviations, mean[:, 1, :],
                                                  ALU.mult, ALU.add))
            chain.settle()
            chain(V.tensor_copy(now[:, :, :], low[:, :, :]))
            chain.restart()

            def count(beside):
                above, not_above = side[:, 0, :], side[:, 1, :]
                pair = lambda mask: mask.unsqueeze(1).to_broadcast([P, 2, TT])
                chain.note(V.tensor_scalar(above, now[:, 1, :], TARGET, None, ALU.is_gt))
                chain(V.tensor_scalar(not_above, now[:, 1, :], TARGET, None, ALU.is_lt))
                chain.note(V.copy_predicated(low[:, :, :], pair(above), now[:, :, :]))
                chain(V.copy_predicated(high[:, :, :], pair(not_above), now[:, :, :]))
                chain(V.tensor_tensor(span[:, :, :], high[:, :, :], low[:, :, :], ALU.subtract))
                chain.note(V.reciprocal(nw[:, 0, 0, :], span[:, 1, :]))
                chain(V.scalar_tensor_tensor(nw[:, 1, 0, :], low[:, 1, :], TARGET, span[:, 0, :],
                                             ALU.subtract, ALU.mult))
                chain(V.tensor_tensor(nw[:, 2, 0, :], nw[:, 0, 0, :], nw[:, 1, 0, :], ALU.mult))
                chain(V.tensor_tensor(now[:, 0, :], low[:, 0, :], nw[:, 2, 0, :], ALU.subtract))
                marks = []
                for i in range(TT):
                    if i >= RT:
                        chain.after(marks[i - RT])
                    chain.note(V.tensor_scalar(junk[i % RT], sim[:, i, :], now[:, 0, i:i + 1], None,
                                               ALU.is_gt, ALU.add, accum_out=now[:, 1, i:i + 1]))
                    marks.append(chain.n)
                    if i in beside:
                        beside[i]()
                chain.settle()

            with dve.Fori(0, COUNTS - 1) as j:
                k = STAGES * j
                count({0: lambda: weight_scale(k),
                       TT // 2 + 1: lambda: (weight_scale(k + 1), rounded(k + 1, 1)),
                       TT - 1: lambda: (weight_scale(k + 2), rounded(k + 2, 2))})
                chain.restart()
            count({})
            chain(V.tensor_scalar(bad[:, :], now[:, 1, :], -TARGET, None, ALU.add))
            chain(V.tensor_tensor(bad[:, :], bad[:, :], bad[:, :], ALU.mult))
            V.tensor_scalar(bad[:, :], bad[:, :], 16.0, None, ALU.is_gt).then_inc(s_searched, 1)
            chain.note(V.tensor_scalar(place[:, :], now[:, 1, :], -1.0, float(KEEP - 1), ALU.mult, ALU.add))
            dve.wait_ge(s_flags, 1)
            chain.note(V.tensor_copy(flags_i[:, 0:TT], bank[6][:, 0:TT]))
            chain(V.tensor_reduce(flags_i[:, TT:TT + 1], bank[6][:, 0:TT], AX.X, ALU.max))
            chain.restart()

            slow = Chain(dve, s_slow)
            any_bad = dve.value_load(flags_i[0:1, TT:TT + 1], min_val=0, max_val=P)
            with dve.If(any_bad > 0):
                with dve.Fori(0, TT) as i:
                    tile_bad = dve.value_load(flags_i[0:1, bass.ds(i, 1)], min_val=0, max_val=P)
                    with dve.If(tile_bad > 0):
                        slow(V.tensor_copy(below[0], row(sim, i)))
                        for n in range(ROUNDS):
                            slow(V.max(m8[:, 0, :], below[0]))
                            if n < ROUNDS - 1:
                                slow(V.match_replace(below[0], m8[:, 0, :], below[0], LOWEST))
                        c = (KEEP - 1) % 8
                        slow(V.tensor_copy(now[:, 0, bass.ds(i, 1)], m8[:, 0, c:c + 1]))
                        slow(V.tensor_scalar(place[:, bass.ds(i, 1)], m8[:, 0, c:c + 1], 0.0, None, ALU.mult))
                        slow.restart()
            V.engine_nop().then_inc(s_searched, 1)

            def clip(k):
                chain(V.tensor_scalar(row(w8, k), row(w8, k), 1.0, -1.0, ALU.min, ALU.max))

            def x1_stats(b):
                for t in range(RT):
                    dve.wait_ge(s_x1, RT + RT * b + t + 1)
                    apart()
                    chain.note(V.bn_stats(row(st[:, 0], RT * b + t), row(x_all, RT * b + t)))

            def batch(b, first=False):
                chain.note(V.tensor_tensor(pick[:, 0], iota_e[:, :].unsqueeze(1).to_broadcast([P, RT, 8]),
                                           place[:, bass.ds(RT * b, RT)].unsqueeze(2).to_broadcast([P, RT, 8]),
                                           ALU.is_equal))
                k = W_ADJ + 2 * b
                weight_scale(k)
                for half in range(2):
                    marks = []
                    for t in (2 * half, 2 * half + 1):
                        chain.note(V.tensor_scalar(below[t % 2], row(sim, RT * b + t),
                                                   now[:, 0, bass.ds(RT * b + t, 1)], LOWEST, ALU.is_gt, ALU.mult))
                        marks.append(chain.n)
                    for t in (2 * half, 2 * half + 1):
                        chain.after(marks[t % 2])
                        chain.note(V.tensor_tensor(below[t % 2], below[t % 2], row(sim, RT * b + t), ALU.add))
                        marks[t % 2] = chain.n
                    for t in (2 * half, 2 * half + 1):
                        chain.after(marks[t % 2])
                        chain.note(V.max(m8[:, t, :], below[t % 2]))
                    chain.settle()
                chain.note(V.tensor_tensor(pick[:, 1], pick[:, 0], m8[:, :, :], ALU.mult))
                if not first:
                    dve.wait_ge(s_diag_used, b)
                    apart()
                for t in range(RT):
                    chain.note(V.tensor_scalar(diag[:, t, :], ident_f[:, :], a1[:, bass.ds(RT * b + t, 1)], None, ALU.mult))
                chain.settle()
                V.engine_nop().then_inc(s_diag, 1)
                chain(V.tensor_reduce(thr[:, :], pick[:, 1], AX.X, ALU.add))
                for t in range(RT):
                    dve.wait_ge(s_sig, RT * b + t + 1)
                    apart()
                    V.scalar_tensor_tensor(sig[:, t, :], row(sim, RT * b + t), thr[:, t:t + 1], sig[:, t, :],
                                           ALU.is_ge, ALU.mult).then_inc(s_adj, 1)
                if not first:
                    x1_stats(b - 1)
                weight_scale(k + 1, source=bank[6])
                rounded(k + 1, 1)
                chain.restart()

            batch(0, first=True)
            with dve.Fori(1, B) as b:
                batch(b)
            x1_stats(B - 1)
            chain.settle()

            mean_var(slice(0, 1))
            inverse_roots(slice(0, 1))
            chain.note(V.tensor_copy(a_ln2[:, :], rstd[:, 0, :]))
            chain(V.scalar_tensor_tensor(b_ln2[:, :], mean[:, 0, :], -1.0, rstd[:, 0, :], ALU.mult, ALU.mult))
            V.engine_nop().then_inc(s_ln2, 1)
            for m in range(3):
                weight_scale(W_REST + m, m, W_REST + 3)
            chain.restart()
            with dve.Fori(0, B // 2) as b2:
                for u in range(2):
                    b = 2 * b2 + u
                    for t in range(RT):
                        dve.wait_ge(s_h, RT * b + t + 1)
                        chain.note(V.tensor_reduce(hm[:, 0, t:t + 1], h_sb[u][:, t, :], AX.X, ALU.max,
                                                   apply_absolute_value=True))
                    chain.settle()
                    chain(V.tensor_scalar(hm[:, 1, :], hm[:, 0, :], EPS, 1.0 / 127.0, ALU.max, ALU.mult))
                    chain.note(V.reciprocal(hm[:, 2, :], hm[:, 1, :]))
                    chain(V.tensor_tensor(hm[:, 3, :], hm[:, 1, :], hm[:, 1, :], ALU.mult))
                    chain.note(V.tensor_tensor(xq_f[:, bass.ds(RT * b, RT), SCALE], hm[:, 3, :], hm[:, 1, :], ALU.mult))
                    marks = []
                    for t in range(RT):
                        dve.wait_ge(s_hT, RT * b + t + 1)
                        chain.note(V.tensor_scalar(h_sb[u][:, t, :], h_sb[u][:, t, :], hm[:, 2, t:t + 1], MAGIC,
                                                   ALU.mult, ALU.add))
                        marks.append(chain.n)
                    for t in range(RT):
                        chain.after(marks[t])
                        chain.note(V.tensor_scalar(row(xq, RT * b + t)[:, 0:H], h_sb[u][:, t, :], MAGIC, 127.0,
                                                   ALU.subtract, ALU.min))
                    chain.settle()
                    V.engine_nop().then_inc(s_h_quant, 1)
                chain.restart()
            dve.wait_ge(s_x1_stored, 16 * B)

            dve.wait_ge(s_logits, 2 + TT)
            flat = lambda n: rt[:, n, :, :].rearrange("p t e -> p (t e)")
            logits = bank[0][:, 0:TT * E].rearrange("p (t e) -> p t e", e=E)
            wide = lambda v: v.unsqueeze(2).to_broadcast([P, TT, E])
            e_wide = iota_e[:, :].unsqueeze(1).to_broadcast([P, TT, E])
            red = small
            chain(V.tensor_reduce(red[:, 0, :], logits, AX.X, ALU.max))
            V.tensor_tensor(rt[:, 1, :, :], logits, wide(red[:, 0, :]), ALU.subtract).then_inc(s_rmax, 1)
            dve.wait_ge(s_exp, 1)
            chain(V.tensor_reduce(red[:, 1, :], rt[:, 2, :, :], AX.X, ALU.add))
            chain(V.reciprocal(red[:, 2, :], red[:, 1, :]))
            chain(V.tensor_tensor(rt[:, 3, :, :], rt[:, 2, :, :], wide(red[:, 2, :]), ALU.mult))
            for c in range(TOPK):
                prob = rt[:, 3 + 4 * c, :, :]
                top = red[:, 3 + c, :]
                chain(V.tensor_reduce(top, prob, AX.X, ALU.max))
                chain(V.tensor_tensor(rt[:, 4 + 4 * c, :, :], prob, wide(top), ALU.is_lt))
                chain(V.tensor_scalar(flat(5 + 4 * c), flat(4 + 4 * c), 100.0, None, ALU.mult))
                chain(V.tensor_tensor(rt[:, 5 + 4 * c, :, :], rt[:, 5 + 4 * c, :, :], e_wide, ALU.add))
                chain(V.tensor_reduce(red[:, 5 + c, :], rt[:, 5 + 4 * c, :, :], AX.X, ALU.min))
                chain(V.tensor_tensor(rt[:, 6 + 4 * c, :, :], wide(red[:, 5 + c, :]), e_wide, ALU.is_equal))
                if c == 0:
                    chain(V.scalar_tensor_tensor(flat(7), flat(6), -2.0, flat(3), ALU.mult, ALU.add))
            V.tensor_tensor(m_b[:, :, :], rt[:, 6, :, :], rt[:, 10, :, :], ALU.add).then_inc(s_choice, 1)
            chain(V.tensor_tensor(red[:, 7, :], red[:, 3, :], red[:, 4, :], ALU.add))
            chain(V.reciprocal(red[:, 2, :], red[:, 7, :]))
            for c in range(TOPK):
                chain.note(V.tensor_tensor(combine[:, :, c], red[:, 3 + c, :], red[:, 2, :], ALU.mult))
            chain.note(V.tensor_scalar(xq_f[:, :, TOKEN], iota_t[:, 0:TT], float(P), iota_p[:, :], ALU.mult, ALU.add))
            chain.settle()
            chain.note(V.tensor_copy(xq_f[:, :, WEIGHT], combine[:, :, 0]))
            dve.wait_ge(s_rank, 1)
            rows, tiles, end = bank[1][:, TT * E:TT * E + E], ends[:, 0, :], ends[:, 2, :]
            chain(V.tensor_scalar(ends_i[:, 1, :], rows, float(P - 1), None, ALU.add))
            chain(V.tensor_scalar(ends_i[:, 0, :], ends_i[:, 1, :], 7, None, ALU.arith_shift_right))
            chain(V.tensor_copy(tiles, ends_i[:, 0, :]))
            chain.note(V.tensor_copy(ends[:, 1, :], tiles))
            chain.note(V.tensor_copy(ends[:, 2, :], tiles))
            chain.settle()
            src, dst = 1, 2
            for step in (1, 2, 4):
                chain.note(V.tensor_copy(ends[:, dst, 0:step], ends[:, src, 0:step]))
                chain(V.tensor_tensor(ends[:, dst, step:E], ends[:, src, step:E], ends[:, src, 0:E - step], ALU.add))
                src, dst = dst, src
            end = ends[:, src, :]
            chain(V.tensor_tensor(first_row[:, :], end, tiles, ALU.subtract))
            chain(V.tensor_scalar(first_row[:, :], first_row[:, :], float(P), None, ALU.mult))
            chain(V.tensor_tensor(rt[:, 11, :, :], bank[1][:, 0:TT * E].rearrange("p (t e) -> p t e", e=E),
                                  first_row[:, :].unsqueeze(1).to_broadcast([P, TT, E]), ALU.add))
            for c in range(TOPK):
                chain.note(V.tensor_tensor(rt[:, 12 + c, :, :], rt[:, 11, :, :], rt[:, 6 + 4 * c, :, :], ALU.mult))
            chain.settle()
            for c in range(TOPK):
                chain.note(V.tensor_reduce(red[:, c, :], rt[:, 12 + c, :, :], AX.X, ALU.add))
            chain.settle()
            for c in range(TOPK):
                chain.note(V.tensor_copy(slots[:, :, c], red[:, c, :]))
            chain.settle()
            V.engine_nop().then_inc(s_slots, 1)
            chain.note(V.tensor_copy(ends_i[:, 0, :], end))
            chain(V.tensor_tensor(past[:, :, 0:E - 1], iota_t[:, :].unsqueeze(2).to_broadcast([P, TILES, E - 1]),
                                  end[:, 0:E - 1].unsqueeze(1).to_broadcast([P, TILES, E - 1]), ALU.is_ge))
            chain(V.tensor_reduce(tab[:, :], past[:, :, 0:E - 1], AX.X, ALU.add))
            chain(V.tensor_copy(tab_i[:, :], tab[:, :]))
            chain(V.tensor_scalar(parity[:, :], tab_i[:, :], 1, None, ALU.bitwise_and))
            two = lambda table, at, u: table[:, at:at + 2 * PAIRS].rearrange("p (j u) -> p j u", u=2)[:, :, u]
            words, part = pair_words[:, 0, 0:PAIRS], pair_words[:, 1, 0:PAIRS]
            for n, (table, at, u, unit) in enumerate(((tab_i, LOOP_FROM, 0, EXPERT_A), (tab_i, LOOP_FROM, 1, EXPERT_B),
                                                      (parity, LOOP_FROM - 2, 0, SLOT_A),
                                                      (parity, LOOP_FROM - 2, 1, SLOT_B))):
                chain(V.tensor_scalar(part if n else words, two(table, at, u), float(unit), None, ALU.mult))
                if n:
                    chain(V.tensor_tensor(words, words, part, ALU.add))
            V.engine_nop().then_inc(s_tables, 1)
            half = TT // 2
            for u in range(2):
                for b in range(u * B // 2, (u + 1) * B // 2):
                    dve.wait_ge(s_w8[1], ADJ_TURN + b + 1)
                    clip(W_ADJ + 2 * b + 1)
                dve.wait_ge(s_scattered[u], 16 * half)
                V.tensor_copy(xq_f[:, u * half:(u + 1) * half, WEIGHT],
                              combine[:, u * half:(u + 1) * half, 1]).then_inc(s_second, 1)
            weight_scale(NW - 1)
            for k, s in ((W_REST + 1, 0), (W_REST + 2, 1), (W_REST, 2), (NW - 1, 2)):
                dve.wait_ge(s_w8[s], LAST_TURN[s] - (1 if k == W_REST else 0))
                clip(k)
            V.engine_nop().then_inc(s_clipped, 1)
            dve.wait_ge(s_wscale, 1 + NW)
            wm = wmean[:, :].rearrange("p (e m) -> p m e", m=MATS)
            chain(V.tensor_tensor(expert_c[:, :], wm[:, 0, :], wm[:, 0, :], ALU.mult))
            chain(V.tensor_tensor(expert_c[:, :], expert_c[:, :], wm[:, 1, :], ALU.mult))
            chain(V.tensor_scalar(expert_d[:, :], wm[:, 2, :], 1.0 / 127.0, None, ALU.mult))
            of_tile = tab[:, :].unsqueeze(2).to_broadcast([P, TILES, E])
            by_expert = lambda v: v.unsqueeze(1).to_broadcast([P, TILES, E])
            for constants, by_tile in ((expert_c[:, :], tile_c), (expert_d[:, :], tile_d)):
                chain(V.tensor_tensor(past[:, :, :], of_tile, by_expert(iota_e[:, :]), ALU.is_equal))
                chain(V.tensor_tensor(past[:, :, :], past[:, :, :], by_expert(constants), ALU.mult))
                chain(V.tensor_reduce(by_tile, past[:, :, :], AX.X, ALU.add))

            def rows_in(i, par):
                dve.wait_ge(s_xr_in[par], 16 * (i // 2) + 16 if isinstance(i, int) else i * 8 + 16 - 8 * par)
                apart()
                V.tensor_copy(payload[:, bass.ds(i, 1), :].rearrange("p a n -> p (a n)"),
                              xr_f[par][:, TOKEN:TOKEN + 2]).then_inc(s_dve_order, 1)
                V.tensor_scalar(fs[par], xr_f[par][:, SCALE:SCALE + 1], tile_c[:, bass.ds(i, 1)], None,
                                ALU.mult).then_inc(s_rows_read, 1)

            def product(i, hf):
                dve.wait_ge(s_sq, 2 * i + hf + 1)
                V.tensor_tensor(act_sb[:, hf * 512:(hf + 1) * 512], bank[2 * hf + 1][:, :], sq_sb[hf],
                                ALU.mult).then_inc(s_act, 1)

            def quantise(i, par):
                top, inv, k = tiny[:, 0:1], tiny[:, 1:2], tiny[:, 2:3]
                dve.wait_ge(s_rows_read, i + 1)
                dve.wait_ge(s_act, 2 * i + 2)
                chain(V.tensor_reduce(top, act_sb, AX.X, ALU.max, apply_absolute_value=True))
                chain(V.tensor_scalar(top, top, fs[par], EPS, ALU.mult, ALU.max))
                chain(V.reciprocal(inv, top))
                chain(V.tensor_scalar(k, inv, fs[par], 127.0, ALU.mult, ALU.mult))
                chain(V.tensor_scalar(act_r, act_sb, k, MAGIC, ALU.mult, ALU.add))
                if not (isinstance(i, int) and i < 2):
                    dve.wait_ge(s_at, i - 1)
                V.tensor_scalar(aq[par], act_r, MAGIC, 127.0, ALU.subtract, ALU.min).then_inc(s_aq, 1)
                if not (isinstance(i, int) and i < 2):
                    dve.wait_ge(s_y_copied, 2 + i - 1)
                V.tensor_scalar(osc[par], top, tile_d[:, bass.ds(i, 1)], payload[:, bass.ds(i, 1), 1],
                                ALU.mult, ALU.mult).then_inc(s_osc, 1)

            def step(i, par, more=True):
                product(i, 0)
                if more:
                    rows_in(i + 1, 1 - par)
                    chain.n += 1
                product(i, 1)
                quantise(i, par)

            rows_in(0, 0)
            chain.n += 1
            step(0, 0)
            step(1, 1)
            chain.restart()
            with dve.Fori(0, PAIRS) as j:
                for u in range(2):
                    step(LOOP_FROM + 2 * j + u, u)
                chain.restart()
            step(TILES - 1, 0, more=False)


_INS = ["x", "ctxT", "wqT", "wkT", "gamma", "routerT", "gateT", "upT", "downT"]


def kernel(**inputs):
    import numpy as np
    import concourse.bacc as bacc
    from concourse import mybir as mb
    from concourse.bass_utils import run_bass_kernel_spmd

    a = {k: np.asarray(v) for k, v in inputs.items()}
    c = np.ascontiguousarray
    gate, up, down = a["L0_ffn_gate_w"], a["L0_ffn_up_w"], a["L0_ffn_down_w"]
    E, I, H = gate.shape
    p = 128

    def blocks(w):
        e, r, k = w.shape
        return c(w.reshape(e, r, k // p, p).transpose(0, 3, 2, 1))

    arrays = {
        "x": c(a["x"]),
        "ctxT": c(a["ctx_512"].transpose(0, 2, 1)),
        "wqT": c(a["L0_xattn_Wq"].T),
        "wkT": c(a["L0_xattn_Wk"].T),
        "gamma": c(a["L0_xattn_gamma_raw"].reshape(1, 1)),
        "routerT": c(a["L0_ffn_router_w"].reshape(E, H // p, p).transpose(2, 1, 0)),
        "gateT": blocks(gate),
        "upT": blocks(up),
        "downT": blocks(down),
    }
    nc = bacc.Bacc("TRN2", target_bir_lowering=False, num_devices=1)
    feed, args = {}, []
    for name in _INS:
        arr = arrays[name]
        feed[name + "_in"] = arr
        args.append(nc.dram_tensor(name + "_in", arr.shape, mb.dt.from_np(arr.dtype), kind="ExternalInput").ap())
    tokens = a["x"].shape[0] * a["x"].shape[1]
    out = nc.dram_tensor("out", [tokens + p, H], mb.dt.float32, kind="ExternalOutput").ap()
    build(nc, *args, out)
    r = run_bass_kernel_spmd(nc, [feed], core_ids=[0])
    return r.results[0]["out"][:tokens].reshape(a["x"].shape)
```
